# Optimizing a Trainium2 kernel written in Bass

```python
import numpy as np
import jax
import jax.numpy as jnp

def _softmax(x, axis=-1):
    return jax.nn.softmax(x, axis=axis)

def _gelu(x):
    return jax.nn.gelu(x, approximate=True)

def _silu(x):
    return jax.nn.silu(x)

def _sigmoid(x):
    return jax.nn.sigmoid(x)

def _layernorm(x, axis=-1, eps=1e-05):
    m = jnp.mean(x, axis=axis, keepdims=True)
    v = jnp.var(x, axis=axis, keepdims=True)
    return (x - m) / jnp.sqrt(v + eps)

def _scatter_add(tgt, idx, src, axis=0):
    return tgt.at[idx].add(src)

def _segment_sum(src, seg, n):
    return jax.ops.segment_sum(src, seg, n)
kernel_name = 'mk_xattn_ffn_d1_seqx_r4_4ab581'

def setup_inputs(seed: int=0):
    np.random.seed(seed)
    _w = jnp.asarray

    def _rec_inputs():
        import jax
        import jax.numpy as jnp
        _rk = jax.random.key(seed)
        x = 7.22e-05 + 1 * jax.random.normal(jax.random.fold_in(_rk, 1), (64, 128, 256), jnp.float32)
        _lenS = 128 - jax.random.randint(jax.random.fold_in(_rk, 7), (64,), 0, max(1, 128 // 4) + 1, jnp.int32)
        _lenS2 = 128 - jax.random.randint(jax.random.fold_in(_rk, 8), (64,), 0, max(1, 128 // 4) + 1, jnp.int32)
        _ctx_1024P = jax.random.normal(jax.random.fold_in(_rk, 11), (64, 16, 256), jnp.float32)
        _ctx_1024c = jax.random.dirichlet(jax.random.fold_in(_rk, 511), 0.3 * jnp.ones((16,), jnp.float32), (64, 128))
        _ctx_1024t = jnp.einsum('bsk,bkd->bsd', _ctx_1024c, _ctx_1024P)
        _ctx_1024t = _ctx_1024t * jax.lax.rsqrt(jnp.mean(jnp.square(_ctx_1024t)) + 1e-12) * 0.953939
        ctx_1024 = 4.13588e-05 + 0.999923 * (_ctx_1024t + 0.3 * jax.random.normal(jax.random.fold_in(_rk, 611), (64, 128, 256), jnp.float32))
        return (x, ctx_1024)
    x, ctx_1024 = _rec_inputs()

    def _L0_xattn_setup():
        import jax, jax.numpy as jnp
        import numpy as np
        B, S, E = (4, 512, 256)
        key = jax.random.key(seed)
        ks = jax.random.split(key, 6)
        scale = 1.0 / np.sqrt(E)
        return {'query': jax.random.normal(ks[0], (B, S, E), dtype=jnp.float32), 'key': jax.random.normal(ks[1], (B, S, E), dtype=jnp.float32), 'value': jax.random.normal(ks[2], (B, S, E), dtype=jnp.float32), 'Wq': jax.random.normal(ks[3], (E, E), dtype=jnp.float32) * scale, 'bq': jnp.zeros((E,), dtype=jnp.float32), 'Wk': jax.random.normal(ks[4], (E, E), dtype=jnp.float32) * scale, 'bk': jnp.zeros((E,), dtype=jnp.float32), 'Wv': jax.random.normal(ks[5], (E, E), dtype=jnp.float32) * scale, 'bv': jnp.zeros((E,), dtype=jnp.float32)}
    _L0_xattn_all = _L0_xattn_setup()
    _L0_xattn_in = {k: v for k, v in _L0_xattn_all.items() if k in ('Wq', 'bq', 'Wk', 'bk', 'Wv', 'bv')}
    del _L0_xattn_all

    def _L0_ffn_setup():
        import jax, jax.numpy as jnp
        import numpy as np
        TOPK = 4
        N_GROUPS = 4
        TOPK_GROUPS = 2
        ROUTE_SCALE = 2.5

        def _gate(x2, Wg):
            T = x2.shape[0]
            E = Wg.shape[0]
            scores = x2 @ Wg.T
            s = jax.nn.sigmoid(scores)
            g = s.reshape(T, N_GROUPS, E // N_GROUPS)
            group_scores = g.max(axis=-1)
            _, gidx = jax.lax.top_k(group_scores, TOPK_GROUPS)
            group_mask = jnp.any(jax.nn.one_hot(gidx, N_GROUPS, dtype=jnp.bool_), axis=1)
            masked = jnp.where(group_mask[:, :, None], g, -jnp.inf).reshape(T, E)
            _, idx = jax.lax.top_k(masked, TOPK)
            w = jnp.take_along_axis(s, idx, axis=1)
            w = w / jnp.sum(w, axis=-1, keepdims=True)
            w = w * ROUTE_SCALE
            return (w.astype(x2.dtype), idx)
        key = jax.random.key(seed)
        ks = jax.random.split(key, 6)
        B, S, D, I, E = (2, 512, 256, 256, 16)
        scale = 0.02
        return {'x': jax.random.normal(ks[0], (B, S, D), dtype=jnp.float32), 'Wg': jax.random.normal(ks[1], (E, D), dtype=jnp.float32) * scale, 'W1': jax.random.normal(ks[2], (E, I, D), dtype=jnp.float32) * scale, 'b1': jnp.zeros((E, I), dtype=jnp.float32), 'W2': jax.random.normal(ks[3], (E, D, I), dtype=jnp.float32) * scale, 'b2': jnp.zeros((E, D), dtype=jnp.float32), 'W3': jax.random.normal(ks[4], (E, I, D), dtype=jnp.float32) * scale, 'b3': jnp.zeros((E, I), dtype=jnp.float32)}
    _L0_ffn_all = _L0_ffn_setup()
    _L0_ffn_in = {k: v for k, v in _L0_ffn_all.items() if k in ('Wg', 'W1', 'b1', 'W2', 'b2', 'W3', 'b3')}
    del _L0_ffn_all
    return {'x': x, 'ctx_1024': ctx_1024, 'L0_xattn_Wq': _L0_xattn_in['Wq'], 'L0_xattn_bq': _L0_xattn_in['bq'], 'L0_xattn_Wk': _L0_xattn_in['Wk'], 'L0_xattn_bk': _L0_xattn_in['bk'], 'L0_xattn_Wv': _L0_xattn_in['Wv'], 'L0_xattn_bv': _L0_xattn_in['bv'], 'L0_ffn_Wg': _L0_ffn_in['Wg'], 'L0_ffn_W1': _L0_ffn_in['W1'], 'L0_ffn_b1': _L0_ffn_in['b1'], 'L0_ffn_W2': _L0_ffn_in['W2'], 'L0_ffn_b2': _L0_ffn_in['b2'], 'L0_ffn_W3': _L0_ffn_in['W3'], 'L0_ffn_b3': _L0_ffn_in['b3']}

def reference(x, ctx_1024, L0_xattn_Wq, L0_xattn_bq, L0_xattn_Wk, L0_xattn_bk, L0_xattn_Wv, L0_xattn_bv, L0_ffn_Wg, L0_ffn_W1, L0_ffn_b1, L0_ffn_W2, L0_ffn_b2, L0_ffn_W3, L0_ffn_b3):
    import jax
    import jax.numpy as jnp

    def _L0_xattn_ref(query, key, value, Wq, bq, Wk, bk, Wv, bv):
        import jax, jax.numpy as jnp
        import numpy as np
        B, S, E = (4, 512, 256)
        q = jnp.einsum('bse,ef->bsf', query, Wq) + bq
        k = jnp.einsum('bse,ef->bsf', key, Wk) + bk
        v = jnp.einsum('bse,ef->bsf', value, Wv) + bv
        divisor = jnp.sqrt(jnp.asarray(q.shape[-1], dtype=jnp.float32))
        scores = jnp.einsum('bqe,bke->bqk', q, k) / divisor
        attn = jax.nn.softmax(scores, axis=-1)
        out = jnp.einsum('bqk,bke->bqe', attn, v)
        return out

    def _L0_ffn_ref(x, Wg, W1, b1, W2, b2, W3, b3):
        import jax, jax.numpy as jnp
        import numpy as np
        TOPK = 4
        N_GROUPS = 4
        TOPK_GROUPS = 2
        ROUTE_SCALE = 2.5

        def _gate(x2, Wg):
            T = x2.shape[0]
            E = Wg.shape[0]
            scores = x2 @ Wg.T
            s = jax.nn.sigmoid(scores)
            g = s.reshape(T, N_GROUPS, E // N_GROUPS)
            group_scores = g.max(axis=-1)
            _, gidx = jax.lax.top_k(group_scores, TOPK_GROUPS)
            group_mask = jnp.any(jax.nn.one_hot(gidx, N_GROUPS, dtype=jnp.bool_), axis=1)
            masked = jnp.where(group_mask[:, :, None], g, -jnp.inf).reshape(T, E)
            _, idx = jax.lax.top_k(masked, TOPK)
            w = jnp.take_along_axis(s, idx, axis=1)
            w = w / jnp.sum(w, axis=-1, keepdims=True)
            w = w * ROUTE_SCALE
            return (w.astype(x2.dtype), idx)
        shape = x.shape
        D = shape[-1]
        x2 = x.reshape(-1, D)
        weights, indices = _gate(x2, Wg)
        E = Wg.shape[0]
        y = jnp.zeros_like(x2)
        for e in range(E):
            we = jnp.sum(weights * (indices == e), axis=-1)
            h = jax.nn.silu(x2 @ W1[e].T + b1[e]) * (x2 @ W3[e].T + b3[e])
            y = y + (h @ W2[e].T + b2[e]) * we[:, None]
        return y.reshape(shape)
    x = x + _L0_xattn_ref(_layernorm(x, axis=-1), ctx_1024, ctx_1024, L0_xattn_Wq, L0_xattn_bq, L0_xattn_Wk, L0_xattn_bk, L0_xattn_Wv, L0_xattn_bv)
    x = x + _L0_ffn_ref(_layernorm(x, axis=-1), L0_ffn_Wg, L0_ffn_W1, L0_ffn_b1, L0_ffn_W2, L0_ffn_b2, L0_ffn_W3, L0_ffn_b3)
    return x

_drawn_inputs = setup_inputs


def setup_inputs(seed=0):
    import zlib

    import numpy as np

    out = dict(_drawn_inputs(seed))
    spreads = {'L0_xattn_bq': (0.0, 0.276),
     'L0_xattn_bk': (0.0, 0.8),
     'L0_xattn_bv': (0.0, 0.1),
     'L0_ffn_b1': (0.0, 0.8),
     'L0_ffn_b2': (0.0, 0.1),
     'L0_ffn_b3': (0.0, 0.8)}
    factors = {'L0_ffn_W1': 2.943, 'L0_ffn_W2': 2.775, 'L0_ffn_W3': 2.923}
    for name, (base, spread) in spreads.items():
        noise = np.random.default_rng([zlib.crc32(name.encode()), seed]).standard_normal(out[name].shape)
        drawn = base * np.exp(spread * noise) if base else spread * noise
        out[name] = jnp.asarray(drawn.astype(out[name].dtype))
    for name, factor in factors.items():
        out[name] = (out[name] * factor).astype(out[name].dtype)
    return out
```

```python
from contextlib import ExitStack

import concourse.bass as bass
from concourse import mybir

F32 = mybir.dt.float32
F16 = mybir.dt.float16
I32 = mybir.dt.int32
ALU = mybir.AluOpType
ACT = mybir.ActivationFunctionType
AX_X = mybir.AxisListType.X

P = 128
GB = 4
TB = 2
TS = 4
WS = 32.0
EPS = 1e-5
TOPK, NGRP, TOPG, ROUTE_SCALE = 4, 4, 2, 2.5
NOWHERE = 40000.0
SENTINEL = 9.0
STAGES = 4


def xattn_moe_kernel(nc, x, ctxT, wqkv, qk_bias, bv, wgT, wexpT, b13, b2, out):
    B, S, D = x.shape
    NE = b2.shape[0]
    DC = D // P
    T = B * S
    NB = T // P
    NG = NB // GB
    GT = GB * P
    EG = NE // NGRP
    W13 = 2 * D
    WE = DC * W13 + DC * D
    TR = TB * P
    NT = T * TOPK // TR + NE
    REG = T + TR
    ROW = 2 * D + 4 * NE
    W_AT, TO_AT = D, D + NE
    SCORE_SCALE = 1.0 / (float(D) ** 0.5)
    assert S == P and DC == 2 and NG % 2 == 0 and NG >= 2 * STAGES and NE == NG and NT % TS == 0 and NE == 16

    x_rows = x.rearrange("(g b) s d -> g s b d", b=GB)
    rows_dram = nc.dram_tensor("expert_rows", [NE * REG + TR, ROW // 2], I32).ap()
    x2_dram = nc.dram_tensor("x2_rows", [T, D], F32).ap()
    y_dram = nc.dram_tensor("y_rows", [T * TOPK, D], F32).ap()
    x2_rows = x2_dram.rearrange("(g b s) d -> g s b d", b=GB, s=P)

    with ExitStack() as stack:
        def sb(name, shape, dt=F32):
            return stack.enter_context(nc.sbuf_tensor(name, shape, dt))

        def sem(name):
            return stack.enter_context(nc.semaphore(name))

        banks = [stack.enter_context(nc.psum_tensor(f"bank{i}", [P, 512], F32)) for i in range(8)]
        ps_turn = banks[0:2]
        ps_proj = banks[2:4]
        ps_score, ps_prob = banks[4], banks[5]
        ps_att = banks[6:8]
        ps_rank, ps_total = ps_score[:, 0:GB * NE], ps_score[:, GB * NE:(GB + 1) * NE]
        ps_xt = banks[0:2]
        ps_h1, ps_h3 = banks[2:4], banks[4:6]
        ps_y = banks[6:8]

        ident = sb("ident", [P, P])
        ident16 = sb("ident16", [P, P], F16)
        before = sb("before", [P, P], F16)
        ones16 = sb("ones16", [P, P], F16)
        half = sb("half", [P, GB])
        lower = sb("lower", [P, NGRP, NGRP])
        first_row = sb("first_row", [P, NE])
        token4 = sb("token4", [P, NB])
        pad_at = sb("pad_at", [P, NE, TB])
        tile_no = sb("tile_no", [1, NT])
        pad_row = sb("pad_row", [P, ROW], F16)

        whi = sb("whi", [P, 3, DC, D], F16)
        wlo = sb("wlo", [P, 3, DC, D], F16)
        qkb = sb("qkb", [P, 2, DC])
        bv_all = sb("bv_all", [P, D])
        wg_raw = sb("wg_raw", [P, DC, NE])
        wg_hi = sb("wg_hi", [P, DC, NE], F16)
        wg_lo = sb("wg_lo", [P, DC, NE], F16)
        stage = sb("stage", [P, 2, WE])
        wexp = sb("wexp", [P, NE, 2, WE], F16)
        b13s = sb("b13s", [P, 2, DC, NE])

        xin = sb("xin", [P, 2, GB, D])
        cin = sb("cin", [P, 2, DC, GT])
        xn = sb("xn", [P, GB, D])
        stat = sb("stat", [P, GB, 6])
        mv = sb("mv", [P, GB, 4])
        veps = sb("veps", [P, GB])
        rstd = sb("rstd", [P, GB])
        lnv, rstd0, newton = sb("lnv", [P, GB]), sb("rstd0", [P, GB]), sb("newton", [P, 2, GB])
        lnv2, rstd02, newton2 = sb("lnv2", [P, GB]), sb("rstd02", [P, GB]), sb("newton2", [P, 2, GB])
        stat2 = sb("stat2", [P, GB, 6])
        mv2 = sb("mv2", [P, GB, 4])
        veps2 = sb("veps2", [P, GB])
        rstd2 = sb("rstd2", [P, GB])
        cT = sb("cT", [P, 2, DC, GT], F16)
        xT = sb("xT", [P, 2, DC, GT], F16)
        qT = sb("qT", [P, 2, DC, GT])
        kv = sb("kv", [P, 2, 2, DC * GT])
        kT = kv[:, 0].rearrange("p q (c t) -> p q c t", c=DC)
        vv = kv[:, 1].rearrange("p q (b d) -> p q b d", b=GB)
        wraw = kv[:, 0].rearrange("p q w -> p (q w)")[:, 0:3 * DC * D].rearrange("p (n c f) -> p n c f", n=3, c=DC)
        b2all = kv[:, :, :, :].rearrange("p a q w -> p (a q w)").rearrange("p (e d) -> p e d", e=NE)
        smax = sb("smax", [P, GB])
        nmax = sb("nmax", [P, GB])
        prob = sb("prob", [P, GB, P])
        psums = sb("psums", [P, GB])
        rinv = sb("rinv", [P, GB])
        pT = sb("pT", [P, GB, P])
        x2 = sb("x2", [P, 2, GB, D])
        x2n = sb("x2n", [P, GB, D])
        rows = sb("rows", [P, 2, GB, ROW], F16)
        rows_f, rows_i = rows[:, :, :, :].bitcast(F32), rows[:, :, :, :].bitcast(I32)
        x2T = sb("x2T", [P, 2, DC, GT], F16)

        gexp = sb("gexp", [P, GB, NE])
        gden = sb("gden", [P, GB, NE])
        sig = sb("sig", [P, GB, NE])
        gmax = sb("gmax", [P, GB, NGRP])
        g_gt = sb("g_gt", [P, GB, NGRP, NGRP])
        g_eq = sb("g_eq", [P, GB, NGRP, NGRP])
        g_tie = sb("g_tie", [P, GB, NGRP, NGRP])
        g_beat = sb("g_beat", [P, GB, NGRP, NGRP])
        g_rank = sb("g_rank", [P, GB, NGRP])
        g_keep = sb("g_keep", [P, GB, NGRP])
        g_drop = sb("g_drop", [P, GB, NGRP])
        s_keep = sb("s_keep", [P, GB, NE])
        cand = sb("cand", [P, GB, NE + 4])
        top = sb("top", [P, GB, 8])
        want = sb("want", [P, GB, 8])
        left = sb("left", [P, GB, NE + 4])
        sel = sb("sel", [P, GB, 2 * NE], F16)
        wsel = sb("wsel", [P, GB, NE])
        wsum = sb("wsum", [P, GB])
        winv = sb("winv", [P, GB])
        suffix = sb("suffix", [P, 4, GB, 2 * NE], F16)
        rankb = sb("rankb", [P, GB, NE])
        key = sb("key", [P, GB, NE])
        top_key = sb("top_key", [P, GB, 8])
        row_at = sb("row_at", [P, 2, GB, TOPK], I32)
        next_row = sb("next_row", [P, NE])
        carrier = sb("carrier", [P, 1])
        pool_carrier = sb("pool_carrier", [P, 1])

        pad_idx = sb("pad_idx", [P, NE, TB], I32)
        cnt = sb("cnt", [1, NE])
        cnt_i = sb("cnt_i", [1, NE], I32)
        tiles_i = sb("tiles_i", [1, NE], I32)
        tiles_f = sb("tiles_f", [1, NE])
        ends = sb("ends", [1, 5, 2 * NE])
        past = stage[:, :, :].rearrange("p q w -> p (q w)")[0:1, 0:NT * NE].rearrange("p (j e) -> p j e", j=NT)
        spare = x2T[:, :, :, :].rearrange("p h c t -> p (h c t)").bitcast(F32)[0:1, 0:4 * NT].rearrange("p (n j) -> p n j", n=4)
        tile_e, tile_b, tile_r, tile_s = (spare[:, k] for k in range(4))
        spare_i = xT[:, :, :, :].rearrange("p h c t -> p (h c t)").bitcast(I32)[0:1, 0:2 * NT].rearrange("p (n j) -> p n j", n=2)
        tile_exp, tile_row = spare_i[:, 0], spare_i[:, 1]

        tin, tin_f, tin_i = (r[:, :, :, :].rearrange("p q (h b) w -> p (q h) b w", b=TB) for r in (rows, rows_f, rows_i))
        wt = sb("wt", [P, 2, TB, 2])
        y_to = sb("y_to", [P, 2, TB], I32)
        xt = cin[:, 1].rearrange("p c t -> p (c t)").bitcast(F16).rearrange("p (q h c t) -> p q h c t", q=2, h=2, c=DC)
        silu = xin[:, 0].rearrange("p b d -> p (b d)").rearrange("p (q c t) -> p q c t", q=2, c=DC)
        hid = xin[:, 1].rearrange("p b d -> p (b d)").rearrange("p (q c t) -> p q c t", q=2, c=DC)
        hT = cin[:, 0].rearrange("p c t -> p (c t)").bitcast(F16).rearrange("p (q h c t) -> p q h c t", q=2, h=2, c=DC)
        ysum = qT[:, 0].rearrange("p c t -> p (c t)").rearrange("p (q b d) -> p q b d", q=2, b=TB)
        yw = qT[:, 1].rearrange("p c t -> p (c t)").rearrange("p (q b d) -> p q b d", q=2, b=TB)

        CB = 2
        NC = NB // CB
        y4 = [kv[:, q].rearrange("p q w -> p (q w)").rearrange("p (b k d) -> p b k d", b=CB, k=TOPK) for q in range(2)]
        x2r = x2[:, 0].rearrange("p b d -> p (b d)").rearrange("p (q b d) -> p q b d", q=2, b=CB)
        res = x2[:, 1].rearrange("p b d -> p (b d)").rearrange("p (q b d) -> p q b d", q=2, b=CB)
        part = xn[:, :, :].rearrange("p b d -> p (b d)").rearrange("p (b k d) -> p b k d", b=CB, k=2)
        part1 = x2n[:, 0:2, :]

        small_in = sem("small_in")
        const_ok, setup_ok, w_ok = sem("const_ok"), sem("setup_ok"), sem("w_ok")
        b2_ok, b2_scaled = sem("b2_ok"), sem("b2_scaled")
        x_in, c_in, e_in = ([sem(f"{n}{k}") for k in range(2)] for n in ("x_in", "c_in", "e_in"))
        x2_out, rows_out = ([sem(f"{n}{k}") for k in range(2)] for n in ("x2_out", "rows_out"))
        stat_ok, mv_ok, veps_ok, rstd_ok = sem("stat_ok"), sem("mv_ok"), sem("veps_ok"), sem("rstd_ok")
        ln_ok, ln2_ok, rstd0_ok, rstd02_ok = sem("ln_ok"), sem("ln2_ok"), sem("rstd0_ok"), sem("rstd02_ok")
        newton_ok, newton2_ok = sem("newton_ok"), sem("newton2_ok")
        xn_ok = sem("xn_ok")
        c_hi, c_lo, x_turned, x_hi, x_lo = sem("c_hi"), sem("c_lo"), sem("x_turned"), sem("x_hi"), sem("x_lo")
        k_done, k_ok, v_done, v_ok, q_done, q_ok = sem("k_done"), sem("k_ok"), sem("v_done"), sem("v_ok"), sem("q_done"), sem("q_ok")
        e_hi, e_lo = sem("e_hi"), sem("e_lo")
        score_done, smax_ok, nmax_ok, prob_ok = sem("score_done"), sem("smax_ok"), sem("nmax_ok"), sem("prob_ok")
        rinv_ok, p_turned, p_ok, att_done, x2_ok = sem("rinv_ok"), sem("p_turned"), sem("p_ok"), sem("att_done"), sem("x2_ok")
        stat2_ok, mv2_ok, veps2_ok, rstd2_ok = sem("stat2_ok"), sem("mv2_ok"), sem("veps2_ok"), sem("rstd2_ok")
        x2n_ok, row_hi, row_lo = sem("x2n_ok"), sem("row_hi"), sem("row_lo")
        x2_turned, x2T_ok, gate_done, gexp_ok = sem("x2_turned"), sem("x2T_ok"), sem("gate_done"), sem("gexp_ok")
        route, rank_done, carried = sem("route"), sem("rank_done"), sem("carried")
        pad_in, spare_in, table, pad_ok, table_ok = sem("pad_in"), sem("spare_in"), sem("table"), sem("pad_ok"), sem("table_ok")
        t_in = [sem(f"t_in{k}") for k in range(TS)]
        wt_ok = sem("wt_ok")
        t_turned, xt_ok, h_done, silu_ok, hid_ok = sem("t_turned"), sem("xt_ok"), sem("h_done"), sem("silu_ok"), sem("hid_ok")
        h_hi, h_lo, y_done, ysum_ok, yw_ok, to_ok = sem("h_hi"), sem("h_lo"), sem("y_done"), sem("ysum_ok"), sem("yw_ok"), sem("to_ok")
        y_out = [sem("y_out0"), sem("y_out1")]
        y_in = [sem("y_in0"), sem("y_in1")]
        x2_in = [sem("x2_in0"), sem("x2_in1")]
        part_ok, part1_ok, part2_ok, res_ok = sem("part_ok"), sem("part1_ok"), sem("part2_ok"), sem("res_ok")
        res_out = [sem("res_out0"), sem("res_out1")]

        SEL_AT, READ_AT, ROUTE_OPS = 18, 30, 33

        def wait(eng, s, value):
            if isinstance(value, int) and value <= 0:
                return
            eng.wait_ge(s, value)

        def arrived(eng, sems, g, par, per=16):
            eng.wait_ge(sems[par], per * (g // 2 + 1) if isinstance(g, int) else (per // 2) * (g - par) + per)

        def settled(eng, sems, g, par, per=16):
            if isinstance(g, int):
                wait(eng, sems[par], per * (g // 2))
            else:
                eng.wait_ge(sems[par], (per // 2) * (g - par))

        def pipeline(eng, step):
            def run(t, odd):
                def at(s, f):
                    if not isinstance(t, int) or 0 <= t - s < NG:
                        f(t - s, (odd + s) % 2)
                step(at)
            for t in range(STAGES):
                run(t, t % 2)
            with eng.Fori(STAGES // 2, NG // 2) as i:
                run(2 * i, 0)
                run(2 * i + 1, 1)
            for t in range(NG, NG + STAGES - 1):
                run(t, t % 2)

        def tiles(eng, body, first=True, last=False):
            if first:
                for j in range(TS):
                    body(j, j)
            with eng.Fori(int(first), NT // TS - int(last)) as i:
                for k in range(TS):
                    body(TS * i + k, k)
            if last:
                for j in range(NT - TS, NT):
                    body(j, j - (NT - TS))

        def tile_arrived(eng, j, slot):
            eng.wait_ge(t_in[slot], 16 * (j // TS + 1) if isinstance(j, int) else (16 // TS) * (j - slot) + 16)

        block = stack.enter_context(nc.Block())

        @block.sync
        def _(sp):
            sp.dma_start(wraw, wqkv).then_inc(small_in, 16)
            sp.dma_start(qkb[:, :, :], qk_bias).then_inc(small_in, 16)
            sp.dma_start(wg_raw[:, :, :], wgT).then_inc(small_in, 16)
            sp.dma_start(b13s[:, :, :, :], b13).then_inc(small_in, 16)
            if True:
                sp.dma_start(bv_all[:, :], bv.rearrange("(a d) -> a d", a=1).broadcast_to([P, D])).then_inc(small_in, 16)

            def load(g, par):
                wait(sp, c_lo, DC * (g - 1))
                sp.dma_start(cin[:, par], ctxT[g]).then_inc(c_in[par], 16)
                wait(sp, x2_ok, GB * (g - 1))
                sp.dma_start(xin[:, par], x_rows[g]).then_inc(x_in[par], 16)
                wait(sp, e_lo, g - 1)
                sp.dma_start(stage[:, par], wexpT[g]).then_inc(e_in[par], 16)
                if isinstance(g, int) and g == 1:
                    sp.wait_ge(setup_ok, 1)
                    for b in range(TB):
                        sp.dma_start(rows_dram[NE * REG + b * P:NE * REG + (b + 1) * P, :], pad_row[:, :].bitcast(I32)).then_inc(spare_in, 16)

            def store(g, par):
                sp.wait_ge(x2_ok, GB * (g + 1))
                sp.dma_start(x2_rows[g], x2[:, par]).then_inc(x2_out[par], 16)

            def step(at):
                at(0, load)
                at(1, store)
            pipeline(sp, step)
            sp.wait_ge(score_done, NG)
            sp.wait_ge(att_done, 2 * NG)
            sp.dma_start(b2all.rearrange("p e d -> p (e d)"),
                         b2.rearrange("(a e) d -> a (e d)", a=1).broadcast_to([P, NE * D])).then_inc(b2_ok, 16)
            for par in range(2):
                sp.wait_ge(x2_out[par], 16 * NG // 2)

            sp.wait_ge(table_ok, 1)
            sp.wait_ge(spare_in, 16 * TB)
            sp.wait_ge(pad_in, 16 * NE * TB)
            for par in range(2):
                sp.wait_ge(rows_out[par], 16 * GB * TOPK * NG // 2)

            def load_tile(j, slot):
                row = sp.value_load(tile_row[0:1, bass.ds(j, 1)], min_val=0, max_val=NE * REG)
                wait(sp, t_turned, j - TS + 1)
                wait(sp, wt_ok, j - TS + 1)
                sp.dma_start(tin_i[:, slot], rows_dram[bass.ds(row, TR), :].rearrange("(b p) w -> p b w", p=P)).then_inc(t_in[slot], 16)
            tiles(sp, load_tile)

            def load_sum(n, par):
                if isinstance(n, int) and n == 0:
                    for k in range(2):
                        sp.wait_ge(y_out[k], 16 * TB * NT // 2)
                wait(sp, part_ok, n - 1)
                sp.dma_start(y4[par].rearrange("p b k d -> p b (k d)"), y_dram[bass.ds(n * (CB * P * TOPK), CB * P * TOPK), :]
                             .rearrange("(b p k) d -> p b (k d)", b=CB, k=TOPK)).then_inc(y_in[par], 16)
                wait(sp, res_ok, n - 1)
                sp.dma_start(x2r[:, par], x2_dram[bass.ds(n * (CB * P), CB * P), :].rearrange("(b p) d -> p b d", p=P)).then_inc(x2_in[par], 16)

            for n in range(2):
                load_sum(n, n)
            with sp.Fori(1, NC // 2) as i:
                load_sum(2 * i, 0)
                load_sum(2 * i + 1, 1)

        @block.gpsimd
        def _(pool):
            n = [0]

            def const(ins):
                n[0] += 1
                ins.then_inc(const_ok, 1)
            pad_f = pad_row[:, :].bitcast(F32)
            const(pool.memset(ident[:, :], 0.0))
            const(pool.memset(before[:, :], 1.0))
            const(pool.memset(lower[:, :, :], 1.0))
            const(pool.memset(ones16[:, :], 1.0))
            const(pool.memset(half[:, :], -0.5))
            const(pool.memset(pad_f[:, 0:TO_AT], 0.0))
            const(pool.iota(pad_f[:, TO_AT:TO_AT + NE], [[0, NE]], base=int(NOWHERE), channel_multiplier=1,
                            allow_small_or_imprecise_dtypes=True))
            const(pool.iota(first_row[:, :], [[1, NE]], base=0, channel_multiplier=0, allow_small_or_imprecise_dtypes=True))
            const(pool.iota(token4[:, :], [[TOPK * P, NB]], base=-1, channel_multiplier=TOPK, allow_small_or_imprecise_dtypes=True))
            const(pool.iota(pad_at[:, :, :], [[0, NE], [P, TB]], base=-1, channel_multiplier=1, allow_small_or_imprecise_dtypes=True))
            const(pool.iota(tile_no[:, :], [[1, NT]], base=0, channel_multiplier=0, allow_small_or_imprecise_dtypes=True))
            pool.wait_ge(const_ok, n[0])
            const(pool.affine_select(out=ident[:, :], in_=ident[:, :], compare_op=ALU.not_equal, fill=1.0, base=0,
                                     pattern=[[-1, P]], channel_multiplier=1))
            const(pool.affine_select(out=before[:, :], in_=before[:, :], compare_op=ALU.is_gt, fill=0.0, base=0,
                                     pattern=[[1, P]], channel_multiplier=-1))
            const(pool.affine_select(out=lower[:, :, :], in_=lower[:, :, :], compare_op=ALU.is_gt, fill=0.0, base=0,
                                     pattern=[[1, NGRP], [-1, NGRP]], channel_multiplier=0))
            const(pool.tensor_scalar(first_row[:, :], first_row[:, :], float(REG), 1.0, ALU.mult, ALU.add))
            pool.wait_ge(const_ok, n[0])
            pool.tensor_copy(ident16[:, :], ident[:, :]).then_inc(setup_ok, 1)

            def carry(k):
                wait(pool, carried, k)
                pool.tensor_tensor(pool_carrier[:, :], half[:, 0:1], half[:, 1:2], ALU.add).then_inc(carried, 1)

            def scatter(g, par):
                pool.wait_ge(route, ROUTE_OPS * (g + 1))
                pool.wait_ge(row_lo, g + 1)
                carry(g)
                for b in range(GB):
                    for k in range(TOPK):
                        pool.indirect_dma_start(rows_dram, bass.IndirectOffsetOnAxis(ap=row_at[:, par, b, k:k + 1], axis=0),
                                                rows_i[:, par, b], None).then_inc(rows_out[par], 16)

            def step(at):
                at(3, scatter)
            pipeline(pool, step)
            pool.wait_ge(pad_ok, 1)
            for e in range(NE):
                for b in range(TB):
                    pool.indirect_dma_start(rows_dram, bass.IndirectOffsetOnAxis(ap=pad_idx[:, e, b:b + 1], axis=0),
                                            pad_row[:, :].bitcast(I32), None).then_inc(pad_in, 16)

            def send(j, slot):
                par = slot % 2
                pool.wait_ge(to_ok, j + 1)
                pool.wait_ge(yw_ok, TB * (j + 1))
                carry(j + NG)
                for b in range(TB):
                    pool.indirect_dma_start(y_dram, bass.IndirectOffsetOnAxis(ap=y_to[:, par, b:b + 1], axis=0),
                                            yw[:, par, b], None, bounds_check=T * TOPK - 1, oob_is_err=False).then_inc(y_out[par], 16)
            tiles(pool, send, first=False)
            for par in range(2):
                pool.wait_ge(y_out[par], 16 * TB * NT // 2)

        @block.scalar
        def _(act):
            act.wait_ge(small_in, 16 * 5)
            act.mul(whi[:, :, :, :], wraw, WS).then_inc(w_ok, 1)
            act.mul(wg_hi[:, :, :], wg_raw[:, :, :], WS).then_inc(w_ok, 1)

            def power(g, par):
                act.wait_ge(veps_ok, g + 1)
                act.activation(lnv[:, :], veps[:, :], ACT.Ln).then_inc(ln_ok, 1)
                act.wait_ge(ln_ok, g + 1)
                act.activation(rstd0[:, :], lnv[:, :], ACT.Exp, scale=-0.5).then_inc(rstd0_ok, 1)

            def power2(g, par):
                act.wait_ge(veps2_ok, g + 1)
                act.activation(lnv2[:, :], veps2[:, :], ACT.Ln).then_inc(ln2_ok, 1)
                act.wait_ge(ln2_ok, g + 1)
                act.activation(rstd02[:, :], lnv2[:, :], ACT.Exp, scale=-0.5).then_inc(rstd02_ok, 1)

            def split_c(g, par):
                arrived(act, c_in, g, par)
                for c in range(DC):
                    wait(act, v_done, 2 * g)
                    act.copy(cT[:, 0, c], cin[:, par, c]).then_inc(c_hi, 1)

            def split_e(g, par):
                arrived(act, e_in, g, par)
                act.mul(wexp[:, bass.ds(g, 1), 0, :].rearrange("p a w -> p (a w)"), stage[:, par], WS).then_inc(e_hi, 1)

            def split_x(g, par):
                for c in range(DC):
                    act.wait_ge(x_turned, DC * g + c + 1)
                    wait(act, q_done, DC * g)
                    act.copy(xT[:, 0, c], ps_turn[c][:, :]).then_inc(x_hi, 1)

            def projections(g, par):
                for c in range(DC):
                    act.wait_ge(k_done, DC * g + c + 1)
                    wait(act, score_done, g - 1)
                    act.activation(kT[:, par, c], ps_proj[c][:, :], ACT.Identity, bias=qkb[:, 1, c:c + 1], scale=1.0 / WS).then_inc(k_ok, 1)
                for c in range(DC):
                    act.wait_ge(q_done, DC * g + c + 1)
                    act.activation(qT[:, par, c], ps_proj[c][:, :], ACT.Identity, bias=qkb[:, 0, c:c + 1], scale=1.0 / WS).then_inc(q_ok, 1)

            def exponentials(g, par):
                act.wait_ge(nmax_ok, g + 1)
                wait(act, p_turned, g)
                wait(act, rinv_ok, g)
                for b in range(GB):
                    act.activation(prob[:, b], ps_score[:, b * P:(b + 1) * P], ACT.Exp, bias=nmax[:, b:b + 1],
                                   scale=SCORE_SCALE, accum_out=psums[:, b:b + 1]).then_inc(prob_ok, 1)

            def copy_p(g, par):
                act.wait_ge(p_turned, g + 1)
                wait(act, att_done, 2 * g)
                act.copy(pT[:, :, :], ps_prob[:, :].rearrange("p (b q) -> p b q", b=GB)).then_inc(p_ok, 1)

            def row_halves(g, par):
                act.wait_ge(x2n_ok, g + 1)
                settled(act, rows_out, g, par, 16 * GB * TOPK)
                act.copy(rows[:, par, :, 0:D], x2n[:, :, :]).then_inc(row_hi, 1)

            def copy_x2T(g, par):
                for h in range(2):
                    act.wait_ge(x2_turned, 2 * g + h + 1)
                    wait(act, gate_done, g)
                    act.copy(x2T[:, :, :, h * 2 * P:(h + 1) * 2 * P],
                             ps_turn[h][:, :].bitcast(F16).rearrange("p (h c t) -> p h c t", h=2, c=DC)).then_inc(x2T_ok, 1)

            def gate(g, par):
                act.wait_ge(gate_done, g + 1)
                wait(act, route, ROUTE_OPS * (g - 1) + SEL_AT)
                act.activation(gexp[:, :, :], ps_prob[:, 0:GB * NE].rearrange("p (b e) -> p b e", b=GB), ACT.Exp,
                               scale=-1.0 / WS).then_inc(gexp_ok, 1)

            def step(at):
                at(0, power)
                at(0, split_c)
                at(2, power2)
                at(1, exponentials)
                at(2, row_halves)
                at(0, split_x)
                at(1, copy_p)
                at(2, copy_x2T)
                at(2, gate)
                at(0, split_e)
                at(0, projections)
            pipeline(act, step)

            act.wait_ge(b2_ok, 16)
            act.mul(b2all, b2all, WS * WS).then_inc(b2_scaled, 1)
            act.wait_ge(table_ok, 1)

            def hidden(j, par):
                e = act.value_load(tile_exp[0:1, bass.ds(j, 1)], min_val=0, max_val=NE - 1)
                act.wait_ge(h_done, j + 1)
                wait(act, hid_ok, DC * (j - 1))
                for c in range(DC):
                    act.activation(silu[:, par, c], ps_h1[par][:, c * TR:(c + 1) * TR], ACT.Silu,
                                   bias=b13s[:, 0, c, bass.ds(e, 1)], scale=1.0 / WS).then_inc(silu_ok, 1)
                act.wait_ge(hid_ok, DC * (j + 1))
                wait(act, y_done, j - 1)
                act.copy(hT[:, par, 0], hid[:, par]).then_inc(h_hi, 1)

            def weigh(j, par):
                act.wait_ge(ysum_ok, j + 1)
                settled(act, y_out, j, par, 16 * TB)
                for b in range(TB):
                    act.mul(yw[:, par, b], ysum[:, par, b], wt[:, par, b, 0:1]).then_inc(yw_ok, 1)
            def tile_step(j, slot):
                hidden(j, slot % 2)
                if not isinstance(j, int) or j:
                    weigh(j - 1, (slot + 1) % 2)
            tiles(act, tile_step)
            weigh(NT - 1, 1)

            def store(n, par):
                act.wait_ge(res_ok, n + 1)
                act.dma_start(out.rearrange("b s d -> (b s) d")[bass.ds(n * (CB * P), CB * P), :].rearrange("(b p) d -> p b d", p=P),
                              res[:, par]).then_inc(res_out[par], 16)
            with act.Fori(0, NC // 2) as i:
                store(2 * i, 0)
                store(2 * i + 1, 1)
            for par in range(2):
                act.wait_ge(res_out[par], 16 * NC // 2)

        @block.vector
        def _(dve):
            dve.memset(cand[:, :, NE:NE + 4], SENTINEL)
            dve.memset(want[:, :, 4:8], SENTINEL)
            dve.memset(sel[:, :, NE:2 * NE], 0.0)
            dve.memset(suffix[:, :, :, :], 0.0)
            dve.memset(ends[:, :, :], 0.0).then_inc(w_ok, 1)
            dve.wait_ge(small_in, 16 * 5)
            dve.wait_ge(w_ok, 3)
            dve.tensor_scalar(b13s[:, 1], b13s[:, 1], WS, None, ALU.mult).then_inc(w_ok, 1)
            for lo_, raw_, hi_ in ((wlo, wraw, whi),):
                dve.scalar_tensor_tensor(out=lo_[:, :, :, :].rearrange("p n c f -> p (n c f)"),
                                         in0=raw_.rearrange("p n c f -> p (n c f)"), scalar=WS,
                                         in1=hi_[:, :, :, :].rearrange("p n c f -> p (n c f)"),
                                         op0=ALU.mult, op1=ALU.subtract).then_inc(w_ok, 1)
            dve.scalar_tensor_tensor(out=wg_lo[:, :, :].rearrange("p c e -> p (c e)"), in0=wg_raw[:, :, :].rearrange("p c e -> p (c e)"),
                                     scalar=WS, in1=wg_hi[:, :, :].rearrange("p c e -> p (c e)"),
                                     op0=ALU.mult, op1=ALU.subtract).then_inc(w_ok, 1)
            dve.wait_ge(setup_ok, 1)
            dve.tensor_copy(next_row[:, :], first_row[:, :]).then_inc(w_ok, 1)

            def moments(st, m, veps_, m_ok, v_ok, g):
                dve.tensor_tensor(m[:, :, 1], st[:, :, 1], st[:, :, 4], ALU.subtract).then_inc(m_ok, 1)
                dve.scalar_tensor_tensor(out=m[:, :, 2], in0=st[:, :, 2], scalar=EPS * D, in1=st[:, :, 5],
                                         op0=ALU.add, op1=ALU.add).then_inc(m_ok, 1)
                dve.wait_ge(m_ok, 4 * g + 2)
                dve.scalar_tensor_tensor(out=m[:, :, 0], in0=m[:, :, 1], scalar=0.5, in1=st[:, :, 4],
                                         op0=ALU.mult, op1=ALU.add).then_inc(m_ok, 1)
                dve.scalar_tensor_tensor(out=m[:, :, 3], in0=m[:, :, 1], scalar=0.25, in1=m[:, :, 1],
                                         op0=ALU.mult, op1=ALU.mult).then_inc(m_ok, 1)
                dve.wait_ge(m_ok, 4 * g + 4)
                dve.scalar_tensor_tensor(out=veps_[:, :], in0=m[:, :, 2], scalar=1.0 / D, in1=m[:, :, 3],
                                         op0=ALU.mult, op1=ALU.add).then_inc(v_ok, 1)

            def refine(y0, y0_ok, v, nw, nw_ok, y, y_ok, g):
                dve.wait_ge(y0_ok, g + 1)
                dve.scalar_tensor_tensor(out=nw[:, 0], in0=y0[:, :], scalar=-0.5, in1=y0[:, :], op0=ALU.mult, op1=ALU.mult).then_inc(nw_ok, 1)
                dve.wait_ge(nw_ok, 2 * g + 1)
                dve.tensor_tensor(nw[:, 1], nw[:, 0], v[:, :], ALU.mult).then_inc(nw_ok, 1)
                dve.wait_ge(nw_ok, 2 * g + 2)
                dve.scalar_tensor_tensor(out=y[:, :], in0=nw[:, 1], scalar=1.5, in1=y0[:, :], op0=ALU.add, op1=ALU.mult).then_inc(y_ok, 1)

            def stats(g, par):
                arrived(dve, x_in, g, par)
                for b in range(GB):
                    dve.bn_stats(stat[:, b], xin[:, par, b]).then_inc(stat_ok, 1)
                dve.wait_ge(stat_ok, GB * (g + 1))
                moments(stat, mv, veps, mv_ok, veps_ok, g)

            def split_c(g, par):
                for c in range(DC):
                    dve.wait_ge(c_hi, DC * g + c + 1)
                    dve.tensor_tensor(cT[:, 1, c], cin[:, par, c], cT[:, 0, c], ALU.subtract).then_inc(c_lo, 1)

            def norm(g, par):
                refine(rstd0, rstd0_ok, veps, newton, newton_ok, rstd, rstd_ok, g)
                dve.wait_ge(rstd_ok, g + 1)
                wait(dve, x_turned, DC * g)
                for b in range(GB):
                    last = dve.tensor_scalar(xn[:, b], xin[:, par, b], mv[:, b, 0:1], rstd[:, b:b + 1],
                                             ALU.subtract, ALU.mult)
                last.then_inc(xn_ok, 1)

            def split_x(g, par):
                for c in range(DC):
                    dve.wait_ge(x_hi, DC * g + c + 1)
                    dve.tensor_tensor(xT[:, 1, c], ps_turn[c][:, :], xT[:, 0, c], ALU.subtract).then_inc(x_lo, 1)

            def split_e(g, par):
                dve.wait_ge(e_hi, g + 1)
                dve.scalar_tensor_tensor(out=wexp[:, bass.ds(g, 1), 1, :].rearrange("p a w -> p (a w)"), in0=stage[:, par], scalar=WS,
                                         in1=wexp[:, bass.ds(g, 1), 0, :].rearrange("p a w -> p (a w)"),
                                         op0=ALU.mult, op1=ALU.subtract).then_inc(e_lo, 1)

            def values(g, par):
                for c in range(2):
                    dve.wait_ge(v_done, 2 * g + c + 1)
                    wait(dve, att_done, 2 * (g - 1))
                    dve.scalar_tensor_tensor(out=vv[:, par, 2 * c:2 * c + 2], in0=ps_proj[c][:, :].rearrange("p (b f) -> p b f", b=2),
                                             scalar=1.0 / WS, in1=bv_all[:, :].rearrange("p (a f) -> p a f", a=1).broadcast_to([P, 2, D]),
                                             op0=ALU.mult, op1=ALU.add).then_inc(v_ok, 1)

            def maxima(g, par):
                dve.wait_ge(score_done, g + 1)
                dve.tensor_reduce(smax[:, :], ps_score[:, :].rearrange("p (b k) -> p b k", b=GB), AX_X, ALU.max).then_inc(smax_ok, 1)
                dve.wait_ge(smax_ok, g + 1)
                wait(dve, prob_ok, GB * g)
                dve.tensor_scalar(nmax[:, :], smax[:, :], -SCORE_SCALE, None, ALU.mult).then_inc(nmax_ok, 1)

            def residual(g, par):
                dve.wait_ge(prob_ok, GB * (g + 1))
                dve.reciprocal(rinv[:, :], psums[:, :]).then_inc(rinv_ok, 1)
                dve.wait_ge(rinv_ok, g + 1)
                settled(dve, x2_out, g, par)
                for b in range(GB):
                    dve.wait_ge(att_done, 2 * g + b // 2 + 1)
                    dve.scalar_tensor_tensor(out=x2[:, par, b], in0=ps_att[b // 2][:, (b % 2) * D:(b % 2 + 1) * D],
                                             scalar=rinv[:, b:b + 1], in1=xin[:, par, b],
                                             op0=ALU.mult, op1=ALU.add).then_inc(x2_ok, 1)

            def stats2(g, par):
                dve.wait_ge(x2_ok, GB * (g + 1))
                for b in range(GB):
                    dve.bn_stats(stat2[:, b], x2[:, par, b]).then_inc(stat2_ok, 1)
                dve.wait_ge(stat2_ok, GB * (g + 1))
                moments(stat2, mv2, veps2, mv2_ok, veps2_ok, g)

            def norm2(g, par):
                refine(rstd02, rstd02_ok, veps2, newton2, newton2_ok, rstd2, rstd2_ok, g)
                dve.wait_ge(rstd2_ok, g + 1)
                wait(dve, row_hi, g)
                for b in range(GB):
                    last = dve.tensor_scalar(x2n[:, b], x2[:, par, b], mv2[:, b, 0:1], rstd2[:, b:b + 1],
                                             ALU.subtract, ALU.mult)
                last.then_inc(x2n_ok, 1)

            def row_halves(g, par):
                dve.wait_ge(row_hi, g + 1)
                dve.tensor_tensor(rows[:, par, :, D:2 * D], x2n[:, :, :], rows[:, par, :, 0:D], ALU.subtract).then_inc(row_lo, 1)

            n = [0]

            def seq(ins):
                n[0] += 1
                return ins.then_inc(route, 1)

            def settle(g):
                dve.wait_ge(route, ROUTE_OPS * g + n[0])

            def over(ap, k):
                return ap

            def choose(g, par):
                n[0] = 0
                dve.wait_ge(gexp_ok, g + 1)
                seq(dve.tensor_scalar(gden[:, :, :], gexp[:, :, :], 1.0, None, ALU.add))
                settle(g)
                seq(dve.reciprocal(sig[:, :, :], gden[:, :, :]))
                settle(g)
                seq(dve.tensor_reduce(gmax[:, :, :], sig[:, :, :].rearrange("p b (g e) -> p b g e", g=NGRP), AX_X, ALU.max))
                settle(g)
                mine = gmax[:, :, :].rearrange("p b (g a) -> p b g a", a=1).broadcast_to([P, GB, NGRP, NGRP])
                other = gmax[:, :, :].rearrange("p b (a h) -> p b a h", a=1).broadcast_to([P, GB, NGRP, NGRP])
                seq(dve.tensor_tensor(g_gt[:, :, :, :], other, mine, ALU.is_gt))
                seq(dve.tensor_tensor(g_eq[:, :, :, :], other, mine, ALU.is_equal))
                settle(g)
                low = lower[:, :, :].rearrange("p g (a h) -> p a g h", a=1).broadcast_to([P, GB, NGRP, NGRP])
                seq(dve.tensor_tensor(g_tie[:, :, :, :], g_eq[:, :, :, :], low, ALU.mult))
                settle(g)
                seq(dve.tensor_tensor(g_beat[:, :, :, :], g_tie[:, :, :, :], g_gt[:, :, :, :], ALU.add))
                settle(g)
                seq(dve.tensor_reduce(g_rank[:, :, :], g_beat[:, :, :, :], AX_X, ALU.add))
                settle(g)
                seq(dve.tensor_scalar(g_keep[:, :, :], g_rank[:, :, :], float(TOPG), None, ALU.is_lt))
                seq(dve.tensor_scalar(g_drop[:, :, :], g_rank[:, :, :], float(TOPG), -1.0, ALU.is_ge, ALU.mult))
                settle(g)

                def spread(t):
                    return t[:, :, :].rearrange("p b (g a) -> p b g a", a=1).broadcast_to([P, GB, NGRP, EG])
                seq(dve.tensor_tensor(s_keep[:, :, :].rearrange("p b (g e) -> p b g e", g=NGRP),
                                      sig[:, :, :].rearrange("p b (g e) -> p b g e", g=NGRP), spread(g_keep), ALU.mult))
                settle(g)
                seq(dve.tensor_tensor(cand[:, :, 0:NE].rearrange("p b (g e) -> p b g e", g=NGRP),
                                      s_keep[:, :, :].rearrange("p b (g e) -> p b g e", g=NGRP), spread(g_drop), ALU.add))
                settle(g)
                seq(dve.memset(carrier[:, :], 0.0))
                for b in range(GB):
                    last = dve.max(top[:, b], cand[:, b, 0:NE])
                seq(last)
                settle(g)
                seq(dve.tensor_copy(want[:, :, 0:TOPK], top[:, :, 0:TOPK]))
                settle(g)
                seq(dve.memset(carrier[:, :], 0.0))
                for b in range(GB):
                    last = dve.match_replace(left[:, b], want[:, b], cand[:, b], -2.0 * SENTINEL)
                seq(last)
                settle(g)
                seq(dve.tensor_scalar(sel[:, :, 0:NE], left[:, :, 0:NE], -SENTINEL, None, ALU.is_lt))
                assert n[0] == SEL_AT, n[0]
                settle(g)
                seq(dve.tensor_tensor(wsel[:, :, :], sig[:, :, :], sel[:, :, 0:NE], ALU.mult))
                seq(dve.tensor_tensor(suffix[:, 0, :, 0:NE], sel[:, :, 0:NE], sel[:, :, 1:NE + 1], ALU.add))
                settle(g)
                seq(dve.tensor_reduce(wsum[:, :], wsel[:, :, :], AX_X, ALU.add))
                for k in range(1, 4):
                    seq(dve.tensor_tensor(suffix[:, k, :, 0:NE], suffix[:, k - 1, :, 0:NE],
                                          suffix[:, k - 1, :, 2 ** k:NE + 2 ** k], ALU.add))
                    settle(g)
                    if k == 1:
                        seq(dve.reciprocal(winv[:, :], wsum[:, :]))
                seq(dve.scalar_tensor_tensor(out=rows_f[:, par, :, W_AT:W_AT + NE], in0=wsel[:, :, :], scalar=ROUTE_SCALE / (WS * WS),
                                             in1=winv[:, :].rearrange("p (b a) -> p b a", a=1).broadcast_to([P, GB, NE]),
                                             op0=ALU.mult, op1=ALU.mult))
                seq(dve.tensor_tensor(rows_f[:, par, :, TO_AT:TO_AT + NE], suffix[:, 3, :, 0:NE],
                                      token4[:, bass.ds(g * GB, GB)].rearrange("p (b a) -> p b a", a=1).broadcast_to([P, GB, NE]),
                                      ALU.add))

            def place(g, par):
                dve.wait_ge(rank_done, g + 1)
                seq(dve.tensor_tensor(rankb[:, :, :], ps_rank.rearrange("p (b e) -> p b e", b=GB),
                                      next_row[:, :].rearrange("p (a e) -> p a e", a=1).broadcast_to([P, GB, NE]), ALU.add))
                settle(g)
                seq(dve.tensor_tensor(key[:, :, :], rankb[:, :, :], sel[:, :, 0:NE], ALU.mult))
                seq(dve.tensor_tensor(next_row[:, :], next_row[:, :], ps_total, ALU.add))
                assert n[0] == READ_AT, n[0]
                settle(g)
                seq(dve.memset(carrier[:, :], 0.0))
                for b in range(GB):
                    last = dve.max(top_key[:, b], key[:, b])
                seq(last)
                settle(g)
                settled(dve, rows_out, g, par, 16 * GB * TOPK)
                seq(dve.tensor_scalar(row_at[:, par], top_key[:, :, 0:TOPK], -1.0, None, ALU.add))
                assert n[0] == ROUTE_OPS, n[0]

            def step(at):
                at(0, stats)
                at(2, stats2)
                at(1, maxima)
                at(0, norm)
                at(0, split_c)
                at(2, norm2)
                at(2, row_halves)
                at(0, split_x)
                at(1, residual)
                at(3, choose)
                at(0, values)
                at(0, split_e)
                at(3, place)
            pipeline(dve, step)

            n[0] = 0

            def tab(ins):
                n[0] += 1
                ins.then_inc(table, 1)
                dve.wait_ge(table, n[0])
            dve.wait_ge(route, ROUTE_OPS * NG)
            dve.tensor_tensor(pad_idx[:, :, :], pad_at[:, :, :], next_row[:, :].rearrange("p (e a) -> p e a", a=1)
                              .broadcast_to([P, NE, TB]), ALU.add).then_inc(pad_ok, 1)
            tab(dve.tensor_tensor(cnt[:, :], next_row[0:1, :], first_row[0:1, :], ALU.subtract))
            tab(dve.tensor_scalar(cnt_i[:, :], cnt[:, :], float(TR - 1), None, ALU.add))
            tab(dve.tensor_scalar(tiles_i[:, :], cnt_i[:, :], TR.bit_length() - 1, None, ALU.arith_shift_right))
            tab(dve.tensor_copy(tiles_f[:, :], tiles_i[:, :]))
            tab(dve.tensor_copy(ends[:, 0, NE:2 * NE], tiles_f[:, :]))
            for k in range(4):
                tab(dve.tensor_tensor(ends[:, k + 1, NE:2 * NE], ends[:, k, NE:2 * NE],
                                      ends[:, k, NE - 2 ** k:2 * NE - 2 ** k], ALU.add))
            tab(dve.tensor_tensor(past[:, :, :], tile_no[:, :].rearrange("p (j a) -> p j a", a=1).broadcast_to([1, NT, NE]),
                                  ends[:, 4, NE:2 * NE].rearrange("p (a e) -> p a e", a=1).broadcast_to([1, NT, NE]), ALU.is_ge))
            tab(dve.tensor_reduce(tile_e, past[:, :, :], AX_X, ALU.add))
            tab(dve.tensor_tensor(past[:, :, :], past[:, :, :],
                                  tiles_f[:, :].rearrange("p (a e) -> p a e", a=1).broadcast_to([1, NT, NE]), ALU.mult))
            tab(dve.tensor_reduce(tile_b, past[:, :, :], AX_X, ALU.add))
            tab(dve.tensor_tensor(tile_r, tile_no[:, :], tile_b, ALU.subtract))
            tab(dve.tensor_scalar(tile_s, tile_e, float(REG), None, ALU.mult))
            tab(dve.scalar_tensor_tensor(out=tile_b, in0=tile_r, scalar=float(TR), in1=tile_s, op0=ALU.mult, op1=ALU.add))
            tab(dve.tensor_scalar(tile_row, tile_b, float(NE * REG), None, ALU.min))
            dve.tensor_scalar(tile_exp, tile_e, float(NE - 1), None, ALU.min).then_inc(table_ok, 1)
            dve.wait_ge(table_ok, 1)
            dve.wait_ge(b2_scaled, 1)

            def copy_xt(j, par):
                dve.wait_ge(t_turned, j + 1)
                wait(dve, h_done, j - 1)
                dve.tensor_copy(xt[:, par], ps_xt[par][:, :].bitcast(F16).rearrange("p (h c t) -> p h c t", h=2, c=DC)).then_inc(xt_ok, 1)

            def copy_wt(j, slot):
                par = slot % 2
                e = dve.value_load(tile_exp[0:1, bass.ds(j, 1)], min_val=0, max_val=NE - 1)
                tile_arrived(dve, j, slot)
                wait(dve, yw_ok, TB * (j - 1))
                wait(dve, to_ok, j - 1)
                dve.tensor_copy(wt[:, par], tin_f[:, slot, :, W_AT:W_AT + 2 * NE].rearrange("p b (s e) -> p b s e", e=NE)
                                [:, :, :, bass.ds(e, 1)].rearrange("p b s a -> p b (s a)")).then_inc(wt_ok, 1)

            def hidden(j, par):
                e = dve.value_load(tile_exp[0:1, bass.ds(j, 1)], min_val=0, max_val=NE - 1)
                for c in range(DC):
                    dve.wait_ge(silu_ok, DC * j + c + 1)
                    if c == 0:
                        wait(dve, h_hi, j - 1)
                    dve.scalar_tensor_tensor(out=hid[:, par, c], in0=ps_h3[par][:, c * TR:(c + 1) * TR],
                                             scalar=b13s[:, 1, c, bass.ds(e, 1)], in1=silu[:, par, c],
                                             op0=ALU.add, op1=ALU.mult).then_inc(hid_ok, 1)

            def low(j, par):
                dve.wait_ge(h_hi, j + 1)
                dve.tensor_tensor(hT[:, par, 1], hid[:, par], hT[:, par, 0], ALU.subtract).then_inc(h_lo, 1)

            def results(j, par):
                e = dve.value_load(tile_exp[0:1, bass.ds(j, 1)], min_val=0, max_val=NE - 1)
                dve.wait_ge(wt_ok, j + 1)
                dve.wait_ge(y_done, j + 1)
                wait(dve, yw_ok, TB * (j - 1))
                dve.tensor_tensor(ysum[:, par], ps_y[par][:, :].rearrange("p (b d) -> p b d", b=TB),
                                  b2all[:, bass.ds(e, 1), :].broadcast_to([P, TB, D]), ALU.add).then_inc(ysum_ok, 1)
                settled(dve, y_out, j, par, 16 * TB)
                dve.tensor_copy(y_to[:, par], wt[:, par, :, 1]).then_inc(to_ok, 1)

            def tile_step(j, slot):
                par = slot % 2
                if not isinstance(j, int) or j + 1 < NT:
                    copy_xt(j + 1, 1 - par)
                hidden(j, par)
                low(j, par)
                copy_wt(j, slot)
                if not isinstance(j, int) or j:
                    results(j - 1, 1 - par)
            copy_xt(0, 0)
            tiles(dve, tile_step, last=True)
            results(NT - 1, 1)

            def last_sum(n, par):
                arrived(dve, y_in, n, par)
                wait(dve, part1_ok, n)
                dve.tensor_tensor(part, y4[par][:, :, 0:2], y4[par][:, :, 2:4], ALU.add).then_inc(part_ok, 1)
                dve.wait_ge(part_ok, n + 1)
                wait(dve, res_ok, n)
                dve.tensor_tensor(part1, part[:, :, 0, :], part[:, :, 1, :], ALU.add).then_inc(part1_ok, 1)
                dve.wait_ge(part1_ok, n + 1)
                arrived(dve, x2_in, n, par)
                settled(dve, res_out, n, par)
                dve.tensor_tensor(res[:, par], part1, x2r[:, par], ALU.add).then_inc(res_ok, 1)
            for n_ in range(2):
                last_sum(n_, n_)
            with dve.Fori(1, NC // 2) as i:
                last_sum(2 * i, 0)
                last_sum(2 * i + 1, 1)

        @block.tensor
        def _(pe):
            pe.wait_ge(setup_ok, 1)
            pe.wait_ge(w_ok, 7)
            PASSES = ((0, 0), (0, 1), (1, 0))
            W = (whi, wlo)
            G = (wg_hi, wg_lo)

            def product(out_ap, pairs):
                for k, (lhs, rhs) in enumerate(pairs):
                    last = pe.matmul(out_ap, lhs, rhs, start=(k == 0), stop=(k == len(pairs) - 1))
                return last

            def scores(g, par):
                pe.wait_ge(q_ok, DC * (g + 1))
                pe.wait_ge(k_ok, DC * (g + 1))
                wait(pe, prob_ok, GB * g)
                wait(pe, route, ROUTE_OPS * (g - 3) + READ_AT)
                for b in range(GB):
                    t = slice(b * P, (b + 1) * P)
                    last = product(ps_score[:, t], [(qT[:, par, c, t], kT[:, par, c, t]) for c in range(DC)])
                last.then_inc(score_done, 1)

            def turn_p(g, par):
                pe.wait_ge(prob_ok, GB * (g + 1))
                wait(pe, p_ok, g)
                wait(pe, gexp_ok, g - 1)
                for b in range(GB):
                    last = pe.transpose(ps_prob[:, b * P:(b + 1) * P], prob[:, b], ident[:, :])
                last.then_inc(p_turned, 1)

            def attend(g, par):
                pe.wait_ge(p_ok, g + 1)
                pe.wait_ge(v_ok, 2 * (g + 1))
                wait(pe, x2_ok, GB * g)
                for b in range(GB):
                    last = product(ps_att[b // 2][:, (b % 2) * D:(b % 2 + 1) * D], [(pT[:, b], vv[:, par, b])])
                    if b % 2:
                        last.then_inc(att_done, 1)

            def turn_x2(g, par):
                pe.wait_ge(row_hi, g + 1)
                pe.wait_ge(row_lo, g + 1)
                for h in range(2):
                    wait(pe, x_lo, DC * (g + 2) + h + 1 if not isinstance(g, int) else min(DC * (g + 2) + h + 1, DC * NG))
                    v = ps_turn[h][:, :].bitcast(F16).rearrange("p (h c t) -> p h c t", h=2, c=DC)
                    for b in range(2):
                        for a in range(2):
                            for c in range(DC):
                                last = pe.transpose(v[:, a, c, b * P:(b + 1) * P],
                                                    rows[:, par, 2 * h + b, a * D + c * P:a * D + (c + 1) * P], ident16[:, :])
                    last.then_inc(x2_turned, 1)

            def gate(g, par):
                pe.wait_ge(x2T_ok, 2 * (g + 1))
                wait(pe, p_ok, g + 2 if not isinstance(g, int) else min(g + 2, NG))
                for b in range(GB):
                    last = product(ps_prob[:, b * NE:(b + 1) * NE],
                                   [(x2T[:, a, c, b * P:(b + 1) * P], G[w][:, c]) for c in range(DC) for a, w in PASSES])
                last.then_inc(gate_done, 1)

            def turn_x(g, par):
                pe.wait_ge(xn_ok, g + 1)
                for c in range(DC):
                    wait(pe, x2T_ok, 2 * (g - 3) + c + 1)
                    wait(pe, x_lo, DC * (g - 1) + c + 1)
                    for b in range(GB):
                        last = pe.transpose(ps_turn[c][:, b * P:(b + 1) * P], xn[:, b, c * P:(c + 1) * P], ident[:, :])
                    last.then_inc(x_turned, 1)

            def project_kv(g, par):
                for f in range(DC):
                    pe.wait_ge(c_lo, DC * (g + 1))
                    wait(pe, q_ok, DC * (g - 1) + f + 1)
                    product(ps_proj[f][:, :], [(W[w][:, 1, c, f * P:(f + 1) * P], cT[:, a, c])
                                               for c in range(DC) for a, w in PASSES]).then_inc(k_done, 1)
                for h in range(2):
                    pe.wait_ge(k_ok, DC * g + h + 1)
                    for b in (2 * h, 2 * h + 1):
                        last = product(ps_proj[h][:, (b % 2) * D:(b % 2 + 1) * D],
                                       [(cT[:, a, c, b * P:(b + 1) * P], W[w][:, 2, c]) for c in range(DC) for a, w in PASSES])
                    last.then_inc(v_done, 1)

            def project_q(g, par):
                pe.wait_ge(x_lo, DC * (g + 1))
                for f in range(DC):
                    pe.wait_ge(v_ok, 2 * g + f + 1)
                    product(ps_proj[f][:, :], [(W[w][:, 0, c, f * P:(f + 1) * P], xT[:, a, c])
                                               for c in range(DC) for a, w in PASSES]).then_inc(q_done, 1)

            def ranks(g, par):
                pe.wait_ge(route, ROUTE_OPS * g + SEL_AT)
                wait(pe, prob_ok, GB * (g + 3) if not isinstance(g, int) else GB * min(g + 3, NG))
                pe.matmul(ps_rank, before[:, :], sel[:, :, 0:NE], start=True, stop=False, skip_group_check=True)
                for b in range(GB - 1):
                    pe.matmul(ps_rank[:, (b + 1) * NE:], ones16[:, :], sel[:, b:b + 1, 0:NE].broadcast_to([P, GB - 1 - b, NE]),
                              start=False, stop=(b == GB - 2), skip_group_check=True)
                for b in range(GB):
                    last = pe.matmul(ps_total, ones16[:, :], sel[:, b, 0:NE], start=(b == 0), stop=(b == GB - 1), skip_group_check=True)
                last.then_inc(rank_done, 1)

            def step(at):
                at(1, scores)
                at(0, turn_x)
                at(1, turn_p)
                at(2, turn_x2)
                at(1, attend)
                at(2, gate)
                at(0, project_kv)
                at(3, ranks)
                at(0, project_q)
            pipeline(pe, step)

            pe.wait_ge(table_ok, 1)

            def turn_tile(j, slot):
                par = slot % 2
                tile_arrived(pe, j, slot)
                wait(pe, xt_ok, j - 1)
                v = ps_xt[par][:, :].bitcast(F16).rearrange("p (h c t) -> p h c t", h=2, c=DC)
                for a in range(2):
                    for c in range(DC):
                        for b in range(TB):
                            last = pe.transpose(v[:, a, c, b * P:(b + 1) * P], tin[:, slot, b, a * D + c * P:a * D + (c + 1) * P], ident16[:, :])
                last.then_inc(t_turned, 1)

            def up(j, par):
                e = pe.value_load(tile_exp[0:1, bass.ds(j, 1)], min_val=0, max_val=NE - 1)
                pe.wait_ge(xt_ok, j + 1)
                wait(pe, hid_ok, DC * (j - 1))
                for m, bank in enumerate((ps_h1[par], ps_h3[par])):
                    for i in range(DC):
                        at = m * D + i * P
                        last = product(bank[:, i * TR:(i + 1) * TR],
                                       [(wexp[:, bass.ds(e, 1), w, c * W13 + at:c * W13 + at + P].rearrange("p a f -> p (a f)"), xt[:, par, a, c])
                                        for c in range(DC) for a, w in PASSES])
                last.then_inc(h_done, 1)

            def down(j, par):
                e = pe.value_load(tile_exp[0:1, bass.ds(j, 1)], min_val=0, max_val=NE - 1)
                pe.wait_ge(h_hi, j + 1)
                pe.wait_ge(h_lo, j + 1)
                wait(pe, ysum_ok, j - 1)
                for b in range(TB):
                    last = product(ps_y[par][:, b * D:(b + 1) * D],
                                   [(hT[:, par, a, c, b * P:(b + 1) * P],
                                     wexp[:, bass.ds(e, 1), w, DC * W13 + c * D:DC * W13 + (c + 1) * D].rearrange("p a f -> p (a f)"))
                                    for c in range(DC) for a, w in PASSES])
                last.then_inc(y_done, 1)

            def tile_step(j, slot):
                if not isinstance(j, int) or j + 1 < NT:
                    turn_tile(j + 1, (slot + 1) % TS)
                up(j, slot % 2)
                if not isinstance(j, int) or j:
                    down(j - 1, (slot + 1) % 2)
            turn_tile(0, 0)
            tiles(pe, tile_step, last=True)
            down(NT - 1, 1)


_OUTS = [((64, 128, 256), 'float32')]


def kernel(**inputs):
    import numpy as _np
    import concourse.bacc as _bacc
    from concourse import mybir as _mybir
    from concourse.bass_utils import run_bass_kernel_spmd as _run

    a = {k: _np.asarray(v) for k, v in inputs.items()}
    E, D = a['L0_ffn_Wg'].shape
    C = D // P

    def chunks(w):
        w = w.reshape(*w.shape[:-2], C, P, w.shape[-1])
        return _np.swapaxes(w, -3, -2).reshape(*w.shape[:-3], P, C * w.shape[-1])

    flip = lambda w: _np.swapaxes(w, -1, -2)
    up = _np.concatenate([flip(a['L0_ffn_W1']), flip(a['L0_ffn_W3'])], axis=-1)
    laid = {
        'x': a['x'],
        'ctxT': a['ctx_1024'].reshape(-1, GB * P, C, P).transpose(0, 3, 2, 1),
        'wqkv': _np.stack([chunks(a[f'L0_xattn_W{n}']).reshape(P, C, D) for n in 'qkv'], axis=1),
        'qk_bias': _np.stack([a['L0_xattn_bq'].reshape(C, P).T, a['L0_xattn_bk'].reshape(C, P).T], axis=1),
        'bv': a['L0_xattn_bv'],
        'wgT': chunks(a['L0_ffn_Wg'].T).reshape(P, C, E),
        'wexpT': _np.concatenate([chunks(up), chunks(flip(a['L0_ffn_W2']))], axis=-1),
        'b13': _np.stack([a[f'L0_ffn_b{n}'].reshape(E, C, P).transpose(2, 1, 0) for n in '13'], axis=1),
        'b2': a['L0_ffn_b2'],
    }
    nc = _bacc.Bacc("TRN2", target_bir_lowering=False, num_devices=1)
    arrays, args = {}, []
    for name, v in laid.items():
        v = _np.ascontiguousarray(v)
        arrays[f"in_{name}_dram"] = v
        args.append(nc.dram_tensor(f"in_{name}_dram", v.shape, _mybir.dt.from_np(v.dtype), kind="ExternalInput").ap())
    for i, (shape, dtype) in enumerate(_OUTS):
        dt = _mybir.dt.from_np(_np.dtype(dtype))
        args.append(nc.dram_tensor(f"out_{i}_dram", shape, dt, kind="ExternalOutput").ap())
    xattn_moe_kernel(nc, *args)
    r = _run(nc, [arrays], core_ids=[0])
    got = tuple(r.results[0][f"out_{i}_dram"] for i in range(len(_OUTS)))
    return got[0]
```

```python
from contextlib import ExitStack

import concourse.bass as bass
from concourse import mybir

F32 = mybir.dt.float32
F16 = mybir.dt.float16
I32 = mybir.dt.int32
ALU = mybir.AluOpType
ACT = mybir.ActivationFunctionType
AX_X = mybir.AxisListType.X

P = 128
GB = 4
TB = 2
TS = 4
WS = 32.0
EPS = 1e-5
TOPK, NGRP, TOPG, ROUTE_SCALE = 4, 4, 2, 2.5
NOWHERE = 40000.0
SENTINEL = 9.0
STAGES = 4


def xattn_moe_kernel(nc, x, ctxT, wqkv, qk_bias, bv, wgT, wexpT, b13, b2, out):
    B, S, D = x.shape
    NE = b2.shape[0]
    DC = D // P
    T = B * S
    NB = T // P
    NG = NB // GB
    GT = GB * P
    EG = NE // NGRP
    W13 = 2 * D
    WE = DC * W13 + DC * D
    TR = TB * P
    NT = T * TOPK // TR + NE
    REG = T + TR
    ROW = 2 * D + 4 * NE
    W_AT, TO_AT = D, D + NE
    SCORE_SCALE = 1.0 / (float(D) ** 0.5)
    assert S == P and DC == 2 and NG % 2 == 0 and NG >= 2 * STAGES and NE == NG and NT % TS == 0 and NE == 16

    x_rows = x.rearrange("(g b) s d -> g s b d", b=GB)
    rows_dram = nc.dram_tensor("expert_rows", [NE * REG + TR, ROW // 2], I32).ap()
    x2_dram = nc.dram_tensor("x2_rows", [T, D], F32).ap()
    y_dram = nc.dram_tensor("y_rows", [T * TOPK, D], F32).ap()
    x2_rows = x2_dram.rearrange("(g b s) d -> g s b d", b=GB, s=P)

    with ExitStack() as stack:
        def sb(name, shape, dt=F32):
            return stack.enter_context(nc.sbuf_tensor(name, shape, dt))

        def sem(name):
            return stack.enter_context(nc.semaphore(name))

        banks = [stack.enter_context(nc.psum_tensor(f"bank{i}", [P, 512], F32)) for i in range(8)]
        ps_turn = banks[0:2]
        ps_proj = banks[2:4]
        ps_score, ps_prob = banks[4], banks[5]
        ps_att = banks[6:8]
        ps_rank, ps_total = ps_score[:, 0:GB * NE], ps_score[:, GB * NE:(GB + 1) * NE]
        ps_xt = banks[0:2]
        ps_h1, ps_h3 = banks[2:4], banks[4:6]
        ps_y = banks[6:8]

        ident = sb("ident", [P, P])
        ident16 = sb("ident16", [P, P], F16)
        before = sb("before", [P, P], F16)
        ones16 = sb("ones16", [P, P], F16)
        half = sb("half", [P, GB])
        lower = sb("lower", [P, NGRP, NGRP])
        first_row = sb("first_row", [P, NE])
        token4 = sb("token4", [P, NB])
        tile_no = sb("tile_no", [1, NT])
        pad_row = sb("pad_row", [P, ROW], F16)

        whi = sb("whi", [P, 3, DC, D], F16)
        wlo = sb("wlo", [P, 3, DC, D], F16)
        qkb = sb("qkb", [P, 2, DC])
        bv_all = sb("bv_all", [P, D])
        wg_raw = sb("wg_raw", [P, DC, NE])
        wg_hi = sb("wg_hi", [P, DC, NE], F16)
        wg_lo = sb("wg_lo", [P, DC, NE], F16)
        stage = sb("stage", [P, 2, WE])
        wexp = sb("wexp", [P, NE, 2, WE], F16)
        b13s = sb("b13s", [P, 2, DC, NE])

        xin = sb("xin", [P, 2, GB, D])
        cin = sb("cin", [P, 2, DC, GT])
        xn = sb("xn", [P, GB, D])
        stat = sb("stat", [P, 2 * GB, 6])
        mean, dif, both, sq = (sb(n, [P, 2 * GB]) for n in ("mean", "dif", "both", "sq"))
        veps = sb("veps", [P, 2 * GB])
        root = sb("root", [P, 5, 2 * GB])
        square, slope = sb("square", [P, 2 * GB]), sb("slope", [P, 2 * GB])
        cT = sb("cT", [P, 2, DC, GT], F16)
        xT = sb("xT", [P, 2, DC, GT], F16)
        qT = sb("qT", [P, 2, DC, GT])
        kv = sb("kv", [P, 2, 2, DC * GT])
        kT = kv[:, 0].rearrange("p q (c t) -> p q c t", c=DC)
        vv = kv[:, 1].rearrange("p q (b d) -> p q b d", b=GB)
        wraw = kv[:, 0].rearrange("p q w -> p (q w)")[:, 0:3 * DC * D].rearrange("p (n c f) -> p n c f", n=3, c=DC)
        b2all = kv[:, :, :, :].rearrange("p a q w -> p (a q w)").rearrange("p (e d) -> p e d", e=NE)
        smax = sb("smax", [P, GB])
        nmax = sb("nmax", [P, GB])
        prob = sb("prob", [P, GB, P])
        psums = sb("psums", [P, GB])
        rinv = sb("rinv", [P, GB])
        pT = sb("pT", [P, GB, P])
        x2 = sb("x2", [P, 2, GB, D])
        x2n = sb("x2n", [P, GB, D])
        rows = sb("rows", [P, 2, GB, ROW], F16)
        root_i, veps_i = root[:, :, :].bitcast(I32), veps[:, :].bitcast(I32)
        rows_f, rows_i = rows[:, :, :, :].bitcast(F32), rows[:, :, :, :].bitcast(I32)
        x2T = sb("x2T", [P, 2, DC, GT], F16)

        gexp = sb("gexp", [P, GB, NE])
        gden = sb("gden", [P, GB, NE])
        sig = sb("sig", [P, GB, NE])
        gmax = sb("gmax", [P, GB, NGRP])
        g_gt = sb("g_gt", [P, GB, NGRP, NGRP])
        g_eq = sb("g_eq", [P, GB, NGRP, NGRP])
        g_tie = sb("g_tie", [P, GB, NGRP, NGRP])
        g_beat = sb("g_beat", [P, GB, NGRP, NGRP])
        g_rank = sb("g_rank", [P, GB, NGRP])
        g_keep = sb("g_keep", [P, GB, NGRP])
        g_drop = sb("g_drop", [P, GB, NGRP])
        s_keep = sb("s_keep", [P, GB, NE])
        cand = sb("cand", [P, GB, NE + 4])
        top = sb("top", [P, GB, 8])
        want = sb("want", [P, GB, 8])
        left = sb("left", [P, GB, NE + 4])
        sel = sb("sel", [P, GB, 2 * NE], F16)
        wsel = sb("wsel", [P, GB, NE])
        wsum = sb("wsum", [P, GB])
        winv = sb("winv", [P, GB])
        suffix = sb("suffix", [P, 4, GB, 2 * NE], F16)
        rankb = sb("rankb", [P, GB, NE])
        key = sb("key", [P, GB, NE])
        top_key = sb("top_key", [P, GB, 8])
        row_at = sb("row_at", [P, 2, GB, TOPK], I32)
        next_row = sb("next_row", [P, NE])
        carrier = sb("carrier", [P, 1])
        pool_carrier = sb("pool_carrier", [P, 1])

        pad_to = sb("pad_to", [1, NE], I32)
        cnt = sb("cnt", [1, NE])
        cnt_i = sb("cnt_i", [1, NE], I32)
        tiles_i = sb("tiles_i", [1, NE], I32)
        tiles_f = sb("tiles_f", [1, NE])
        ends = sb("ends", [1, 5, 2 * NE])
        past = stage[:, :, :].rearrange("p q w -> p (q w)")[0:1, 0:NT * NE].rearrange("p (j e) -> p j e", j=NT)
        spare = x2T[:, :, :, :].rearrange("p h c t -> p (h c t)").bitcast(F32)[0:1, 0:4 * NT].rearrange("p (n j) -> p n j", n=4)
        tile_e, tile_b, tile_r, tile_s = (spare[:, k] for k in range(4))
        spare_i = xT[:, :, :, :].rearrange("p h c t -> p (h c t)").bitcast(I32)[0:1, 0:2 * (TS + NT)].rearrange("p (n j) -> p n j", n=2)
        tile_exp, tile_row = spare_i[:, 0], spare_i[:, 1]

        tin, tin_f, tin_i = (r[:, :, :, :].rearrange("p q (h b) w -> p (q h) b w", b=TB) for r in (rows, rows_f, rows_i))
        wt = sb("wt", [P, 2, TB, 2])
        y_to = sb("y_to", [P, 2, TB], I32)
        xt = cin[:, 1].rearrange("p c t -> p (c t)").bitcast(F16).rearrange("p (q h c t) -> p q h c t", q=2, h=2, c=DC)
        silu = xin[:, 0].rearrange("p b d -> p (b d)").rearrange("p (q c t) -> p q c t", q=2, c=DC)
        hid = xin[:, 1].rearrange("p b d -> p (b d)").rearrange("p (q c t) -> p q c t", q=2, c=DC)
        hT = cin[:, 0].rearrange("p c t -> p (c t)").bitcast(F16).rearrange("p (q h c t) -> p q h c t", q=2, h=2, c=DC)
        ysum = qT[:, 0].rearrange("p c t -> p (c t)").rearrange("p (q b d) -> p q b d", q=2, b=TB)
        yw = qT[:, 1].rearrange("p c t -> p (c t)").rearrange("p (q b d) -> p q b d", q=2, b=TB)

        CB = 2
        NC = NB // CB
        y4 = [kv[:, q].rearrange("p q w -> p (q w)").rearrange("p (b k d) -> p b k d", b=CB, k=TOPK) for q in range(2)]
        x2r = x2[:, 0].rearrange("p b d -> p (b d)").rearrange("p (q b d) -> p q b d", q=2, b=CB)
        res = x2[:, 1].rearrange("p b d -> p (b d)").rearrange("p (q b d) -> p q b d", q=2, b=CB)
        part = xn[:, :, :].rearrange("p b d -> p (b d)").rearrange("p (b k d) -> p b k d", b=CB, k=2)
        part1 = x2n[:, 0:2, :]

        small_in = sem("small_in")
        const_ok, setup_ok, w_ok = sem("const_ok"), sem("setup_ok"), sem("w_ok")
        b2_ok, b2_scaled = sem("b2_ok"), sem("b2_scaled")
        x_in, c_in, e_in = ([sem(f"{n}{k}") for k in range(2)] for n in ("x_in", "c_in", "e_in"))
        x_again, x2_out, rows_out = ([sem(f"{n}{k}") for k in range(2)] for n in ("x_again", "x2_out", "rows_out"))
        stat_ok, stat2_ok, root_ok = sem("stat_ok"), sem("stat2_ok"), sem("root_ok")
        xn_ok = sem("xn_ok")
        c_hi, c_lo, x_turned, x_hi, x_lo = sem("c_hi"), sem("c_lo"), sem("x_turned"), sem("x_hi"), sem("x_lo")
        k_done, k_ok, v_done, v_ok, q_done, q_ok = sem("k_done"), sem("k_ok"), sem("v_done"), sem("v_ok"), sem("q_done"), sem("q_ok")
        e_hi, e_lo = sem("e_hi"), sem("e_lo")
        score_done, smax_ok, nmax_ok, prob_ok = sem("score_done"), sem("smax_ok"), sem("nmax_ok"), sem("prob_ok")
        rinv_ok, p_turned, p_ok, att_done, x2_ok = sem("rinv_ok"), sem("p_turned"), sem("p_ok"), sem("att_done"), sem("x2_ok")
        x2n_ok, row_hi, row_lo = sem("x2n_ok"), sem("row_hi"), sem("row_lo")
        x2_turned, x2T_ok, gate_done, gexp_ok = sem("x2_turned"), sem("x2T_ok"), sem("gate_done"), sem("gexp_ok")
        route, rank_done, carried = sem("route"), sem("rank_done"), sem("carried")
        pad_in, spare_in, table, pad_ok, table_ok = sem("pad_in"), sem("spare_in"), sem("table"), sem("pad_ok"), sem("table_ok")
        t_in = [sem(f"t_in{k}") for k in range(TS)]
        wt_ok = sem("wt_ok")
        t_turned, xt_ok, h_done, silu_ok, hid_ok = sem("t_turned"), sem("xt_ok"), sem("h_done"), sem("silu_ok"), sem("hid_ok")
        h_hi, h_lo, y_done, ysum_ok, yw_ok, to_ok = sem("h_hi"), sem("h_lo"), sem("y_done"), sem("ysum_ok"), sem("yw_ok"), sem("to_ok")
        y_out = [sem("y_out0"), sem("y_out1")]
        y_in = [sem("y_in0"), sem("y_in1")]
        x2_in = [sem("x2_in0"), sem("x2_in1")]
        part_ok, part1_ok, part2_ok, res_ok = sem("part_ok"), sem("part1_ok"), sem("part2_ok"), sem("res_ok")
        res_out = [sem("res_out0"), sem("res_out1")]

        SEL_AT, READ_AT, ROUTE_OPS = 18, 30, 33
        ROOT_OPS = 16
        REFINEMENTS = 3

        def wait(eng, s, value):
            if isinstance(value, int) and value <= 0:
                return
            eng.wait_ge(s, value)

        def arrived(eng, sems, g, par, per=16):
            eng.wait_ge(sems[par], per * (g // 2 + 1) if isinstance(g, int) else (per // 2) * (g - par) + per)

        def settled(eng, sems, g, par, per=16):
            if isinstance(g, int):
                wait(eng, sems[par], per * (g // 2))
            else:
                eng.wait_ge(sems[par], (per // 2) * (g - par))

        def pipeline(eng, step):
            def run(t, odd):
                def at(s, f):
                    if not isinstance(t, int) or 0 <= t - s < NG:
                        f(t - s, (odd + s) % 2)
                step(at, t)
            for t in range(-1, STAGES):
                run(t, t % 2)
            with eng.Fori(STAGES // 2, NG // 2 - 1) as i:
                run(2 * i, 0)
                run(2 * i + 1, 1)
            for t in range(NG - 2, NG + STAGES - 1):
                run(t, t % 2)

        def tiles(eng, body, first=True, last=False, with_experts=True):
            rounds = []

            def round_(j0):
                if with_experts:
                    regs = [eng.alloc_register(f"expert{n}_{len(rounds)}") for n in range(2 * TS)]
                    rounds.append(j0)
                    eng.load(regs, tile_exp[0:1, bass.ds(j0, 2 * TS)])
                    experts = [eng.snap(reg, donate=True, min_val=0, max_val=NE - 1) for reg in regs]
                for k in range(TS):
                    body(j0 + k, k, (lambda n, k=k: experts[TS + k - n]) if with_experts else None)
            if first:
                round_(0)
            with eng.Fori(int(first), NT // TS - int(last)) as i:
                round_(TS * i)
            if last:
                round_(NT - TS)

        def tile_arrived(eng, j, slot):
            eng.wait_ge(t_in[slot], 16 * (j // TS + 1) if isinstance(j, int) else (16 // TS) * (j - slot) + 16)

        block = stack.enter_context(nc.Block())

        @block.sync
        def _(sp):
            sp.dma_start(wraw, wqkv).then_inc(small_in, 16)
            sp.dma_start(qkb[:, :, :], qk_bias).then_inc(small_in, 16)
            sp.dma_start(wg_raw[:, :, :], wgT).then_inc(small_in, 16)
            sp.dma_start(b13s[:, :, :, :], b13).then_inc(small_in, 16)
            if True:
                sp.dma_start(bv_all[:, :], bv.rearrange("(a d) -> a d", a=1).broadcast_to([P, D])).then_inc(small_in, 16)

            def load(g, par):
                wait(sp, c_lo, DC * (g - 1))
                sp.dma_start(cin[:, par], ctxT[g]).then_inc(c_in[par], 16)
                wait(sp, xn_ok, g - 1)
                sp.dma_start(xin[:, par], x_rows[g]).then_inc(x_in[par], 16)
                wait(sp, e_lo, g - 1)
                sp.dma_start(stage[:, par], wexpT[g]).then_inc(e_in[par], 16)
                if isinstance(g, int) and g == 1:
                    sp.wait_ge(setup_ok, 1)
                    for b in range(TB):
                        sp.dma_start(rows_dram[NE * REG + b * P:NE * REG + (b + 1) * P, :], pad_row[:, :].bitcast(I32)).then_inc(spare_in, 16)

            def load_again(g, par):
                settled(sp, x2_out, g, par)
                wait(sp, x2n_ok, GB * (g - 1))
                sp.dma_start(x2[:, par], x_rows[g]).then_inc(x_again[par], 16)

            def store(g, par):
                sp.wait_ge(x2_ok, GB * (g + 1))
                sp.dma_start(x2_rows[g], x2[:, par]).then_inc(x2_out[par], 16)

            def step(at, t):
                at(-1, load)
                at(0, load_again)
                at(1, store)
            pipeline(sp, step)
            sp.wait_ge(pad_ok, 1)
            for e in range(NE):
                row = sp.value_load(pad_to[0:1, e:e + 1], min_val=0, max_val=NE * REG)
                sp.dma_start(rows_dram[bass.ds(row, TR), :].rearrange("(b p) w -> p b w", p=P),
                             pad_row[:, :].bitcast(I32).rearrange("p (a w) -> p a w", a=1).broadcast_to([P, TB, ROW // 2])).then_inc(pad_in, 16)
            for par in range(2):
                sp.wait_ge(x2_out[par], 16 * NG // 2)

            sp.wait_ge(table_ok, 1)
            sp.wait_ge(spare_in, 16 * TB)
            sp.wait_ge(pad_in, 16 * NE)
            for par in range(2):
                sp.wait_ge(rows_out[par], 16 * GB * TOPK * NG // 2)

            def load_tile(j, slot, _):
                row = sp.value_load(tile_row[0:1, bass.ds(j + TS, 1)], min_val=0, max_val=NE * REG)
                wait(sp, t_turned, j - TS + 1)
                wait(sp, wt_ok, j - TS + 1)
                sp.dma_start(tin_i[:, slot], rows_dram[bass.ds(row, TR), :].rearrange("(b p) w -> p b w", p=P)).then_inc(t_in[slot], 16)
            tiles(sp, load_tile, with_experts=False)

            def load_sum(n, par):
                if isinstance(n, int) and n == 0:
                    for k in range(2):
                        sp.wait_ge(y_out[k], 16 * TB * NT // 2)
                wait(sp, part_ok, n - 1)
                sp.dma_start(y4[par].rearrange("p b k d -> p b (k d)"), y_dram[bass.ds(n * (CB * P * TOPK), CB * P * TOPK), :]
                             .rearrange("(b p k) d -> p b (k d)", b=CB, k=TOPK)).then_inc(y_in[par], 16)
                wait(sp, res_ok, n - 1)
                sp.dma_start(x2r[:, par], x2_dram[bass.ds(n * (CB * P), CB * P), :].rearrange("(b p) d -> p b d", p=P)).then_inc(x2_in[par], 16)

            for n in range(2):
                load_sum(n, n)
            with sp.Fori(1, NC // 2) as i:
                load_sum(2 * i, 0)
                load_sum(2 * i + 1, 1)

        @block.gpsimd
        def _(pool):
            n = [0]

            def const(ins):
                n[0] += 1
                ins.then_inc(const_ok, 1)
            pad_f = pad_row[:, :].bitcast(F32)
            const(pool.memset(ident[:, :], 0.0))
            const(pool.memset(before[:, :], 1.0))
            const(pool.memset(lower[:, :, :], 1.0))
            const(pool.memset(ones16[:, :], 1.0))
            const(pool.memset(half[:, :], -0.5))
            const(pool.memset(pad_f[:, 0:TO_AT], 0.0))
            const(pool.iota(pad_f[:, TO_AT:TO_AT + NE], [[0, NE]], base=int(NOWHERE), channel_multiplier=1,
                            allow_small_or_imprecise_dtypes=True))
            const(pool.iota(first_row[:, :], [[1, NE]], base=0, channel_multiplier=0, allow_small_or_imprecise_dtypes=True))
            const(pool.iota(token4[:, :], [[TOPK * P, NB]], base=-1, channel_multiplier=TOPK, allow_small_or_imprecise_dtypes=True))
            const(pool.iota(tile_no[:, :], [[1, NT]], base=0, channel_multiplier=0, allow_small_or_imprecise_dtypes=True))
            pool.wait_ge(const_ok, n[0])
            const(pool.affine_select(out=ident[:, :], in_=ident[:, :], compare_op=ALU.not_equal, fill=1.0, base=0,
                                     pattern=[[-1, P]], channel_multiplier=1))
            const(pool.affine_select(out=before[:, :], in_=before[:, :], compare_op=ALU.is_gt, fill=0.0, base=0,
                                     pattern=[[1, P]], channel_multiplier=-1))
            const(pool.affine_select(out=lower[:, :, :], in_=lower[:, :, :], compare_op=ALU.is_gt, fill=0.0, base=0,
                                     pattern=[[1, NGRP], [-1, NGRP]], channel_multiplier=0))
            const(pool.tensor_scalar(first_row[:, :], first_row[:, :], float(REG), 1.0, ALU.mult, ALU.add))
            pool.wait_ge(const_ok, n[0])
            pool.tensor_copy(ident16[:, :], ident[:, :]).then_inc(setup_ok, 1)

            def carry(k):
                wait(pool, carried, k)
                pool.tensor_tensor(pool_carrier[:, :], half[:, 0:1], half[:, 1:2], ALU.add).then_inc(carried, 1)

            def scatter(g, par):
                pool.wait_ge(route, ROUTE_OPS * (g + 1))
                pool.wait_ge(row_lo, g + 1)
                carry(g)
                for b in range(GB):
                    for k in range(TOPK):
                        pool.indirect_dma_start(rows_dram, bass.IndirectOffsetOnAxis(ap=row_at[:, par, b, k:k + 1], axis=0),
                                                rows_i[:, par, b], None).then_inc(rows_out[par], 16)

            def step(at, t):
                at(3, scatter)
            pipeline(pool, step)
            def send(j, slot, _):
                par = slot % 2
                pool.wait_ge(to_ok, j + 1)
                pool.wait_ge(yw_ok, TB * (j + 1))
                carry(j + NG)
                for b in range(TB):
                    pool.indirect_dma_start(y_dram, bass.IndirectOffsetOnAxis(ap=y_to[:, par, b:b + 1], axis=0),
                                            yw[:, par, b], None, bounds_check=T * TOPK - 1, oob_is_err=False).then_inc(y_out[par], 16)
            tiles(pool, send, first=False, with_experts=False)
            for par in range(2):
                pool.wait_ge(y_out[par], 16 * TB * NT // 2)

        @block.scalar
        def _(act):
            act.wait_ge(small_in, 16 * 5)
            act.mul(whi[:, :, :, :], wraw, WS).then_inc(w_ok, 1)
            act.mul(wg_hi[:, :, :], wg_raw[:, :, :], WS).then_inc(w_ok, 1)

            def split_c(g, par):
                arrived(act, c_in, g, par)
                for c in range(DC):
                    wait(act, v_done, 2 * g)
                    act.copy(cT[:, 0, c], cin[:, par, c]).then_inc(c_hi, 1)

            def split_e(g, par):
                arrived(act, e_in, g, par)
                act.mul(wexp[:, bass.ds(g, 1), 0, :].rearrange("p a w -> p (a w)"), stage[:, par], WS).then_inc(e_hi, 1)

            def split_x(g, par):
                for c in range(DC):
                    act.wait_ge(x_turned, DC * g + c + 1)
                    wait(act, q_done, DC * g)
                    act.copy(xT[:, 0, c], ps_turn[c][:, :]).then_inc(x_hi, 1)

            def keys(g, par):
                for c in range(DC):
                    act.wait_ge(k_done, DC * g + c + 1)
                    wait(act, score_done, g - 1)
                    act.activation(kT[:, par, c], ps_proj[c][:, :], ACT.Identity, bias=qkb[:, 1, c:c + 1], scale=1.0 / WS).then_inc(k_ok, 1)

            def queries(g, par):
                for c in range(DC):
                    act.wait_ge(q_done, DC * g + c + 1)
                    act.activation(qT[:, par, c], ps_proj[c][:, :], ACT.Identity, bias=qkb[:, 0, c:c + 1], scale=1.0 / WS).then_inc(q_ok, 1)

            def exponentials(g, par):
                act.wait_ge(nmax_ok, g + 1)
                wait(act, p_turned, g)
                wait(act, rinv_ok, g)
                for b in range(GB):
                    act.activation(prob[:, b], ps_score[:, b * P:(b + 1) * P], ACT.Exp, bias=nmax[:, b:b + 1],
                                   scale=SCORE_SCALE, accum_out=psums[:, b:b + 1]).then_inc(prob_ok, 1)

            def copy_p(g, par):
                act.wait_ge(p_turned, g + 1)
                wait(act, att_done, 2 * g)
                act.copy(pT[:, :, :], ps_prob[:, :].rearrange("p (b q) -> p b q", b=GB)).then_inc(p_ok, 1)

            def row_halves(g, par):
                act.wait_ge(x2n_ok, GB * (g + 1))
                settled(act, rows_out, g, par, 16 * GB * TOPK)
                act.copy(rows[:, par, :, 0:D], x2n[:, :, :]).then_inc(row_hi, 1)

            def copy_x2T(g, par):
                for h in range(2):
                    act.wait_ge(x2_turned, 2 * g + h + 1)
                    wait(act, gate_done, g)
                    act.copy(x2T[:, :, :, h * 2 * P:(h + 1) * 2 * P],
                             ps_turn[h][:, :].bitcast(F16).rearrange("p (h c t) -> p h c t", h=2, c=DC)).then_inc(x2T_ok, 1)

            def gate(g, par):
                act.wait_ge(gate_done, g + 1)
                wait(act, route, ROUTE_OPS * (g - 1) + SEL_AT)
                act.activation(gexp[:, :, :], ps_prob[:, 0:GB * NE].rearrange("p (b e) -> p b e", b=GB), ACT.Exp,
                               scale=-1.0 / WS).then_inc(gexp_ok, 1)

            def step(at, t):
                at(0, split_c)
                at(0, split_x)
                at(1, exponentials)
                at(0, keys)
                at(1, copy_p)
                at(0, split_e)
                at(2, row_halves)
                at(0, queries)
                at(2, copy_x2T)
                at(2, gate)
            pipeline(act, step)

            act.wait_ge(score_done, NG)
            act.wait_ge(att_done, 2 * NG)
            act.dma_start(b2all.rearrange("p e d -> p (e d)"),
                          b2.rearrange("(a e) d -> a (e d)", a=1).broadcast_to([P, NE * D])).then_inc(b2_ok, 16)
            act.wait_ge(b2_ok, 16)
            act.mul(b2all, b2all, WS * WS).then_inc(b2_scaled, 1)
            act.wait_ge(table_ok, 1)

            def hidden(j, slot, e):
                par = slot % 2
                act.wait_ge(h_done, j + 1)
                wait(act, hid_ok, DC * (j - 1))
                for c in range(DC):
                    act.activation(silu[:, par, c], ps_h1[par][:, c * TR:(c + 1) * TR], ACT.Silu,
                                   bias=b13s[:, 0, c, bass.ds(e, 1)], scale=1.0 / WS).then_inc(silu_ok, 1)

            def copy_wt(j, slot, e):
                tile_arrived(act, j, slot)
                wait(act, yw_ok, TB * (j - 1))
                wait(act, to_ok, j - 1)
                act.copy(wt[:, slot % 2], tin_f[:, slot, :, W_AT:W_AT + 2 * NE].rearrange("p b (s e) -> p b s e", e=NE)
                         [:, :, :, bass.ds(e, 1)].rearrange("p b s a -> p b (s a)")).then_inc(wt_ok, 1)

            def high(j, slot):
                act.wait_ge(hid_ok, DC * (j + 1))
                wait(act, y_done, j - 1)
                act.copy(hT[:, slot % 2, 0], hid[:, slot % 2]).then_inc(h_hi, 1)

            def weigh(j, par):
                act.wait_ge(wt_ok, j + 1)
                act.wait_ge(ysum_ok, j + 1)
                settled(act, y_out, j, par, 16 * TB)
                for b in range(TB):
                    act.mul(yw[:, par, b], ysum[:, par, b], wt[:, par, b, 0:1]).then_inc(yw_ok, 1)

            def tile_step(j, slot, expert):
                hidden(j, slot, expert(0))
                if not isinstance(j, int) or j >= 2:
                    weigh(j - 2, slot % 2)
                copy_wt(j, slot, expert(0))
                high(j, slot)
            tiles(act, tile_step)
            weigh(NT - 2, 0)
            weigh(NT - 1, 1)

            def store(n, par):
                act.wait_ge(res_ok, n + 1)
                act.dma_start(out.rearrange("b s d -> (b s) d")[bass.ds(n * (CB * P), CB * P), :].rearrange("(b p) d -> p b d", p=P),
                              res[:, par]).then_inc(res_out[par], 16)
            with act.Fori(0, NC // 2) as i:
                store(2 * i, 0)
                store(2 * i + 1, 1)
            for par in range(2):
                act.wait_ge(res_out[par], 16 * NC // 2)

        @block.vector
        def _(dve):
            dve.memset(cand[:, :, NE:NE + 4], SENTINEL)
            dve.memset(want[:, :, 4:8], SENTINEL)
            dve.memset(stat[:, :, :], 0.0)
            dve.memset(sel[:, :, NE:2 * NE], 0.0)
            dve.memset(suffix[:, :, :, :], 0.0)
            dve.memset(ends[:, :, :], 0.0).then_inc(w_ok, 1)
            dve.wait_ge(small_in, 16 * 5)
            dve.wait_ge(w_ok, 3)
            dve.tensor_scalar(b13s[:, 1], b13s[:, 1], WS, None, ALU.mult).then_inc(w_ok, 1)
            for lo_, raw_, hi_ in ((wlo, wraw, whi),):
                dve.scalar_tensor_tensor(out=lo_[:, :, :, :].rearrange("p n c f -> p (n c f)"),
                                         in0=raw_.rearrange("p n c f -> p (n c f)"), scalar=WS,
                                         in1=hi_[:, :, :, :].rearrange("p n c f -> p (n c f)"),
                                         op0=ALU.mult, op1=ALU.subtract).then_inc(w_ok, 1)
            dve.scalar_tensor_tensor(out=wg_lo[:, :, :].rearrange("p c e -> p (c e)"), in0=wg_raw[:, :, :].rearrange("p c e -> p (c e)"),
                                     scalar=WS, in1=wg_hi[:, :, :].rearrange("p c e -> p (c e)"),
                                     op0=ALU.mult, op1=ALU.subtract).then_inc(w_ok, 1)
            dve.wait_ge(setup_ok, 1)
            dve.tensor_copy(next_row[:, :], first_row[:, :]).then_inc(w_ok, 1)

            def stats(g, par):
                arrived(dve, x_in, g, par)
                for b in range(GB):
                    dve.bn_stats(stat[:, b], xin[:, par, b]).then_inc(stat_ok, 1)

            def stats2(g, par):
                dve.wait_ge(x2_ok, GB * (g + 1))
                for b in range(GB):
                    dve.bn_stats(stat[:, GB + b], x2[:, par, b]).then_inc(stat2_ok, 1)

            def inverse_deviations(t):
                ops = [0]

                def seq(ins):
                    ops[0] += 1
                    ins.then_inc(root_ok, 1)

                def settle():
                    dve.wait_ge(root_ok, ROOT_OPS * (t + 1) + ops[0])
                if not isinstance(t, int) or t + 1 < NG:
                    dve.wait_ge(stat_ok, GB * (t + 2))
                if not isinstance(t, int) or t >= 1:
                    dve.wait_ge(stat2_ok, GB * t)
                seq(dve.tensor_tensor(dif[:, :], stat[:, :, 1], stat[:, :, 4], ALU.subtract))
                seq(dve.scalar_tensor_tensor(out=both[:, :], in0=stat[:, :, 2], scalar=EPS * D, in1=stat[:, :, 5],
                                             op0=ALU.add, op1=ALU.add))
                settle()
                seq(dve.scalar_tensor_tensor(out=mean[:, :], in0=dif[:, :], scalar=0.5, in1=stat[:, :, 4], op0=ALU.mult, op1=ALU.add))
                seq(dve.scalar_tensor_tensor(out=sq[:, :], in0=dif[:, :], scalar=0.25, in1=dif[:, :], op0=ALU.mult, op1=ALU.mult))
                settle()
                seq(dve.scalar_tensor_tensor(out=veps[:, :], in0=both[:, :], scalar=1.0 / D, in1=sq[:, :], op0=ALU.mult, op1=ALU.add))
                settle()
                seq(dve.tensor_scalar(root_i[:, 4], veps_i, 1, None, ALU.arith_shift_right))
                settle()
                seq(dve.tensor_scalar(root_i[:, 0], root_i[:, 4], -1.0, float(0x5F3759DF), ALU.mult, ALU.add))
                for k in range(REFINEMENTS):
                    settle()
                    seq(dve.scalar_tensor_tensor(out=square[:, :], in0=root[:, k], scalar=-0.5, in1=root[:, k], op0=ALU.mult, op1=ALU.mult))
                    settle()
                    seq(dve.tensor_tensor(slope[:, :], square[:, :], veps[:, :], ALU.mult))
                    settle()
                    seq(dve.scalar_tensor_tensor(out=root[:, k + 1], in0=slope[:, :], scalar=1.5, in1=root[:, k], op0=ALU.add, op1=ALU.mult))
                assert ops[0] == ROOT_OPS, ops[0]

            def split_c(g, par):
                for c in range(DC):
                    dve.wait_ge(c_hi, DC * g + c + 1)
                    dve.tensor_tensor(cT[:, 1, c], cin[:, par, c], cT[:, 0, c], ALU.subtract).then_inc(c_lo, 1)

            def norm(g, par):
                dve.wait_ge(root_ok, ROOT_OPS * (g + 1))
                wait(dve, x_turned, DC * g)
                for b in range(GB):
                    last = dve.tensor_scalar(xn[:, b], xin[:, par, b], mean[:, b:b + 1], root[:, REFINEMENTS, b:b + 1],
                                             ALU.subtract, ALU.mult)
                last.then_inc(xn_ok, 1)

            def split_x(g, par):
                for c in range(DC):
                    dve.wait_ge(x_hi, DC * g + c + 1)
                    dve.tensor_tensor(xT[:, 1, c], ps_turn[c][:, :], xT[:, 0, c], ALU.subtract).then_inc(x_lo, 1)

            def split_e(g, par):
                dve.wait_ge(e_hi, g + 1)
                dve.scalar_tensor_tensor(out=wexp[:, bass.ds(g, 1), 1, :].rearrange("p a w -> p (a w)"), in0=stage[:, par], scalar=WS,
                                         in1=wexp[:, bass.ds(g, 1), 0, :].rearrange("p a w -> p (a w)"),
                                         op0=ALU.mult, op1=ALU.subtract).then_inc(e_lo, 1)

            def values(g, par):
                for c in range(2):
                    dve.wait_ge(v_done, 2 * g + c + 1)
                    wait(dve, att_done, 2 * (g - 1))
                    dve.scalar_tensor_tensor(out=vv[:, par, 2 * c:2 * c + 2], in0=ps_proj[c][:, :].rearrange("p (b f) -> p b f", b=2),
                                             scalar=1.0 / WS, in1=bv_all[:, :].rearrange("p (a f) -> p a f", a=1).broadcast_to([P, 2, D]),
                                             op0=ALU.mult, op1=ALU.add).then_inc(v_ok, 1)

            def maxima(g, par):
                dve.wait_ge(score_done, g + 1)
                dve.tensor_reduce(smax[:, :], ps_score[:, :].rearrange("p (b k) -> p b k", b=GB), AX_X, ALU.max).then_inc(smax_ok, 1)
                dve.wait_ge(smax_ok, g + 1)
                wait(dve, prob_ok, GB * g)
                dve.tensor_scalar(nmax[:, :], smax[:, :], -SCORE_SCALE, None, ALU.mult).then_inc(nmax_ok, 1)

            def residual(g, par):
                dve.wait_ge(prob_ok, GB * (g + 1))
                dve.reciprocal(rinv[:, :], psums[:, :]).then_inc(rinv_ok, 1)
                dve.wait_ge(rinv_ok, g + 1)
                arrived(dve, x_again, g, par)
                for b in range(GB):
                    dve.wait_ge(att_done, 2 * g + b // 2 + 1)
                    dve.scalar_tensor_tensor(out=x2[:, par, b], in0=ps_att[b // 2][:, (b % 2) * D:(b % 2 + 1) * D],
                                             scalar=rinv[:, b:b + 1], in1=x2[:, par, b],
                                             op0=ALU.mult, op1=ALU.add).then_inc(x2_ok, 1)

            def norm2(g, par):
                dve.wait_ge(root_ok, ROOT_OPS * (g + 3))
                wait(dve, row_hi, g)
                for b in range(GB):
                    dve.tensor_scalar(x2n[:, b], x2[:, par, b], mean[:, GB + b:GB + b + 1], root[:, REFINEMENTS, GB + b:GB + b + 1],
                                      ALU.subtract, ALU.mult).then_inc(x2n_ok, 1)

            def row_halves(g, par):
                dve.wait_ge(row_hi, g + 1)
                dve.tensor_tensor(rows[:, par, :, D:2 * D], x2n[:, :, :], rows[:, par, :, 0:D], ALU.subtract).then_inc(row_lo, 1)

            n = [0]

            def seq(ins):
                n[0] += 1
                return ins.then_inc(route, 1)

            def settle(g):
                dve.wait_ge(route, ROUTE_OPS * g + n[0])

            def choose(g, par):
                n[0] = 0
                dve.wait_ge(gexp_ok, g + 1)
                seq(dve.tensor_scalar(gden[:, :, :], gexp[:, :, :], 1.0, None, ALU.add))
                settle(g)
                seq(dve.reciprocal(sig[:, :, :], gden[:, :, :]))
                settle(g)
                seq(dve.tensor_reduce(gmax[:, :, :], sig[:, :, :].rearrange("p b (g e) -> p b g e", g=NGRP), AX_X, ALU.max))
                settle(g)
                mine = gmax[:, :, :].rearrange("p b (g a) -> p b g a", a=1).broadcast_to([P, GB, NGRP, NGRP])
                other = gmax[:, :, :].rearrange("p b (a h) -> p b a h", a=1).broadcast_to([P, GB, NGRP, NGRP])
                seq(dve.tensor_tensor(g_gt[:, :, :, :], other, mine, ALU.is_gt))
                seq(dve.tensor_tensor(g_eq[:, :, :, :], other, mine, ALU.is_equal))
                settle(g)
                low = lower[:, :, :].rearrange("p g (a h) -> p a g h", a=1).broadcast_to([P, GB, NGRP, NGRP])
                seq(dve.tensor_tensor(g_tie[:, :, :, :], g_eq[:, :, :, :], low, ALU.mult))
                settle(g)
                seq(dve.tensor_tensor(g_beat[:, :, :, :], g_tie[:, :, :, :], g_gt[:, :, :, :], ALU.add))
                settle(g)
                seq(dve.tensor_reduce(g_rank[:, :, :], g_beat[:, :, :, :], AX_X, ALU.add))
                settle(g)
                seq(dve.tensor_scalar(g_keep[:, :, :], g_rank[:, :, :], float(TOPG), None, ALU.is_lt))
                seq(dve.tensor_scalar(g_drop[:, :, :], g_rank[:, :, :], float(TOPG), -1.0, ALU.is_ge, ALU.mult))
                settle(g)

                def spread(t):
                    return t[:, :, :].rearrange("p b (g a) -> p b g a", a=1).broadcast_to([P, GB, NGRP, EG])
                seq(dve.tensor_tensor(s_keep[:, :, :].rearrange("p b (g e) -> p b g e", g=NGRP),
                                      sig[:, :, :].rearrange("p b (g e) -> p b g e", g=NGRP), spread(g_keep), ALU.mult))
                settle(g)
                seq(dve.tensor_tensor(cand[:, :, 0:NE].rearrange("p b (g e) -> p b g e", g=NGRP),
                                      s_keep[:, :, :].rearrange("p b (g e) -> p b g e", g=NGRP), spread(g_drop), ALU.add))
                settle(g)
                seq(dve.memset(carrier[:, :], 0.0))
                for b in range(GB):
                    last = dve.max(top[:, b], cand[:, b, 0:NE])
                seq(last)
                settle(g)
                seq(dve.tensor_copy(want[:, :, 0:TOPK], top[:, :, 0:TOPK]))
                settle(g)
                seq(dve.memset(carrier[:, :], 0.0))
                for b in range(GB):
                    last = dve.match_replace(left[:, b], want[:, b], cand[:, b], -2.0 * SENTINEL)
                seq(last)
                settle(g)
                seq(dve.tensor_scalar(sel[:, :, 0:NE], left[:, :, 0:NE], -SENTINEL, None, ALU.is_lt))
                assert n[0] == SEL_AT, n[0]
                settle(g)
                seq(dve.tensor_tensor(wsel[:, :, :], sig[:, :, :], sel[:, :, 0:NE], ALU.mult))
                seq(dve.tensor_tensor(suffix[:, 0, :, 0:NE], sel[:, :, 0:NE], sel[:, :, 1:NE + 1], ALU.add))
                settle(g)
                seq(dve.tensor_reduce(wsum[:, :], wsel[:, :, :], AX_X, ALU.add))
                for k in range(1, 4):
                    seq(dve.tensor_tensor(suffix[:, k, :, 0:NE], suffix[:, k - 1, :, 0:NE],
                                          suffix[:, k - 1, :, 2 ** k:NE + 2 ** k], ALU.add))
                    settle(g)
                    if k == 1:
                        seq(dve.reciprocal(winv[:, :], wsum[:, :]))
                seq(dve.scalar_tensor_tensor(out=rows_f[:, par, :, W_AT:W_AT + NE], in0=wsel[:, :, :], scalar=ROUTE_SCALE / (WS * WS),
                                             in1=winv[:, :].rearrange("p (b a) -> p b a", a=1).broadcast_to([P, GB, NE]),
                                             op0=ALU.mult, op1=ALU.mult))
                seq(dve.tensor_tensor(rows_f[:, par, :, TO_AT:TO_AT + NE], suffix[:, 3, :, 0:NE],
                                      token4[:, bass.ds(g * GB, GB)].rearrange("p (b a) -> p b a", a=1).broadcast_to([P, GB, NE]),
                                      ALU.add))

            def place(g, par):
                dve.wait_ge(rank_done, g + 1)
                seq(dve.tensor_tensor(rankb[:, :, :], ps_rank.rearrange("p (b e) -> p b e", b=GB),
                                      next_row[:, :].rearrange("p (a e) -> p a e", a=1).broadcast_to([P, GB, NE]), ALU.add))
                settle(g)
                seq(dve.tensor_tensor(key[:, :, :], rankb[:, :, :], sel[:, :, 0:NE], ALU.mult))
                seq(dve.tensor_tensor(next_row[:, :], next_row[:, :], ps_total, ALU.add))
                assert n[0] == READ_AT, n[0]
                settle(g)
                seq(dve.memset(carrier[:, :], 0.0))
                for b in range(GB):
                    last = dve.max(top_key[:, b], key[:, b])
                seq(last)
                settle(g)
                settled(dve, rows_out, g, par, 16 * GB * TOPK)
                seq(dve.tensor_scalar(row_at[:, par], top_key[:, :, 0:TOPK], -1.0, None, ALU.add))
                assert n[0] == ROUTE_OPS, n[0]

            def step(at, t):
                at(0, norm)
                at(0, split_c)
                at(1, maxima)
                at(2, norm2)
                at(0, split_x)
                at(3, choose)
                at(0, values)
                at(3, place)
                at(2, row_halves)
                at(1, residual)
                at(1, stats2)
                at(-1, stats)
                if not isinstance(t, int) or t <= NG:
                    inverse_deviations(t)
                at(0, split_e)
            pipeline(dve, step)

            n[0] = 0

            def tab(ins):
                n[0] += 1
                ins.then_inc(table, 1)
                dve.wait_ge(table, n[0])
            dve.wait_ge(route, ROUTE_OPS * NG)
            dve.tensor_scalar(pad_to[:, :], next_row[0:1, :], -1.0, None, ALU.add).then_inc(pad_ok, 1)
            tab(dve.tensor_tensor(cnt[:, :], next_row[0:1, :], first_row[0:1, :], ALU.subtract))
            tab(dve.tensor_scalar(cnt_i[:, :], cnt[:, :], float(TR - 1), None, ALU.add))
            tab(dve.tensor_scalar(tiles_i[:, :], cnt_i[:, :], TR.bit_length() - 1, None, ALU.arith_shift_right))
            tab(dve.tensor_copy(tiles_f[:, :], tiles_i[:, :]))
            tab(dve.tensor_copy(ends[:, 0, NE:2 * NE], tiles_f[:, :]))
            for k in range(4):
                tab(dve.tensor_tensor(ends[:, k + 1, NE:2 * NE], ends[:, k, NE:2 * NE],
                                      ends[:, k, NE - 2 ** k:2 * NE - 2 ** k], ALU.add))
            tab(dve.tensor_tensor(past[:, :, :], tile_no[:, :].rearrange("p (j a) -> p j a", a=1).broadcast_to([1, NT, NE]),
                                  ends[:, 4, NE:2 * NE].rearrange("p (a e) -> p a e", a=1).broadcast_to([1, NT, NE]), ALU.is_ge))
            tab(dve.tensor_reduce(tile_e, past[:, :, :], AX_X, ALU.add))
            tab(dve.tensor_tensor(past[:, :, :], past[:, :, :],
                                  tiles_f[:, :].rearrange("p (a e) -> p a e", a=1).broadcast_to([1, NT, NE]), ALU.mult))
            tab(dve.tensor_reduce(tile_b, past[:, :, :], AX_X, ALU.add))
            tab(dve.tensor_tensor(tile_r, tile_no[:, :], tile_b, ALU.subtract))
            tab(dve.tensor_scalar(tile_s, tile_e, float(REG), None, ALU.mult))
            tab(dve.scalar_tensor_tensor(out=tile_b, in0=tile_r, scalar=float(TR), in1=tile_s, op0=ALU.mult, op1=ALU.add))
            tab(dve.tensor_scalar(tile_row[:, TS:TS + NT], tile_b, float(NE * REG), None, ALU.min))
            tab(dve.memset(tile_exp[:, 0:TS], 0))
            dve.tensor_scalar(tile_exp[:, TS:TS + NT], tile_e, float(NE - 1), None, ALU.min).then_inc(table_ok, 1)
            dve.wait_ge(table_ok, 1)
            dve.wait_ge(b2_scaled, 1)

            def copy_xt(j, par):
                dve.wait_ge(t_turned, j + 1)
                wait(dve, h_done, j - 1)
                dve.tensor_copy(xt[:, par], ps_xt[par][:, :].bitcast(F16).rearrange("p (h c t) -> p h c t", h=2, c=DC)).then_inc(xt_ok, 1)

            def hidden(j, par, e):
                for c in range(DC):
                    dve.wait_ge(silu_ok, DC * j + c + 1)
                    if c == 0:
                        wait(dve, h_hi, j - 1)
                    dve.scalar_tensor_tensor(out=hid[:, par, c], in0=ps_h3[par][:, c * TR:(c + 1) * TR],
                                             scalar=b13s[:, 1, c, bass.ds(e, 1)], in1=silu[:, par, c],
                                             op0=ALU.add, op1=ALU.mult).then_inc(hid_ok, 1)

            def low_half(j, par):
                dve.wait_ge(h_hi, j + 1)
                dve.tensor_tensor(hT[:, par, 1], hid[:, par], hT[:, par, 0], ALU.subtract).then_inc(h_lo, 1)

            def results(j, par, e):
                dve.wait_ge(y_done, j + 1)
                wait(dve, yw_ok, TB * (j - 1))
                dve.tensor_tensor(ysum[:, par], ps_y[par][:, :].rearrange("p (b d) -> p b d", b=TB),
                                  b2all[:, bass.ds(e, 1), :].broadcast_to([P, TB, D]), ALU.add).then_inc(ysum_ok, 1)
                dve.wait_ge(wt_ok, j + 1)
                settled(dve, y_out, j, par, 16 * TB)
                dve.tensor_copy(y_to[:, par], wt[:, par, :, 1]).then_inc(to_ok, 1)

            def tile_step(j, slot, expert):
                par = slot % 2
                done = not isinstance(j, int) or j >= 2
                if not isinstance(j, int) or j >= 1:
                    low_half(j - 1, 1 - par)
                if not isinstance(j, int) or j + 1 < NT:
                    copy_xt(j + 1, 1 - par)
                if done:
                    results(j - 2, par, expert(2))
                hidden(j, par, expert(0))
            copy_xt(0, 0)
            tiles(dve, tile_step, last=True)
            low_half(NT - 1, 1)
            for j in (NT - 2, NT - 1):
                results(j, j % 2, dve.value_load(tile_exp[0:1, j + TS:j + TS + 1], min_val=0, max_val=NE - 1))

            def last_sum(n, par):
                arrived(dve, y_in, n, par)
                wait(dve, part1_ok, n)
                dve.tensor_tensor(part, y4[par][:, :, 0:2], y4[par][:, :, 2:4], ALU.add).then_inc(part_ok, 1)
                dve.wait_ge(part_ok, n + 1)
                wait(dve, res_ok, n)
                dve.tensor_tensor(part1, part[:, :, 0, :], part[:, :, 1, :], ALU.add).then_inc(part1_ok, 1)
                dve.wait_ge(part1_ok, n + 1)
                arrived(dve, x2_in, n, par)
                settled(dve, res_out, n, par)
                dve.tensor_tensor(res[:, par], part1, x2r[:, par], ALU.add).then_inc(res_ok, 1)
            for n_ in range(2):
                last_sum(n_, n_)
            with dve.Fori(1, NC // 2) as i:
                last_sum(2 * i, 0)
                last_sum(2 * i + 1, 1)

        @block.tensor
        def _(pe):
            pe.wait_ge(setup_ok, 1)
            pe.wait_ge(w_ok, 7)
            PASSES = ((0, 0), (0, 1), (1, 0))
            W = (whi, wlo)
            G = (wg_hi, wg_lo)

            def product(out_ap, pairs):
                for k, (lhs, rhs) in enumerate(pairs):
                    last = pe.matmul(out_ap, lhs, rhs, start=(k == 0), stop=(k == len(pairs) - 1))
                return last

            def scores(g, par):
                pe.wait_ge(q_ok, DC * (g + 1))
                pe.wait_ge(k_ok, DC * (g + 1))
                wait(pe, prob_ok, GB * g)
                wait(pe, route, ROUTE_OPS * (g - 3) + READ_AT)
                for b in range(GB):
                    t = slice(b * P, (b + 1) * P)
                    last = product(ps_score[:, t], [(qT[:, par, c, t], kT[:, par, c, t]) for c in range(DC)])
                last.then_inc(score_done, 1)

            def turn_p(g, par):
                pe.wait_ge(prob_ok, GB * (g + 1))
                wait(pe, p_ok, g)
                wait(pe, gexp_ok, g - 1)
                for b in range(GB):
                    last = pe.transpose(ps_prob[:, b * P:(b + 1) * P], prob[:, b], ident[:, :])
                last.then_inc(p_turned, 1)

            def attend(g, par):
                pe.wait_ge(p_ok, g + 1)
                pe.wait_ge(v_ok, 2 * (g + 1))
                wait(pe, x2_ok, GB * g)
                for b in range(GB):
                    last = product(ps_att[b // 2][:, (b % 2) * D:(b % 2 + 1) * D], [(pT[:, b], vv[:, par, b])])
                    if b % 2:
                        last.then_inc(att_done, 1)

            def turn_x2(g, par):
                pe.wait_ge(row_hi, g + 1)
                pe.wait_ge(row_lo, g + 1)
                for h in range(2):
                    wait(pe, x_lo, DC * (g + 2) + h + 1 if not isinstance(g, int) else min(DC * (g + 2) + h + 1, DC * NG))
                    v = ps_turn[h][:, :].bitcast(F16).rearrange("p (h c t) -> p h c t", h=2, c=DC)
                    for b in range(2):
                        for a in range(2):
                            for c in range(DC):
                                last = pe.transpose(v[:, a, c, b * P:(b + 1) * P],
                                                    rows[:, par, 2 * h + b, a * D + c * P:a * D + (c + 1) * P], ident16[:, :])
                    last.then_inc(x2_turned, 1)

            def gate(g, par):
                pe.wait_ge(x2T_ok, 2 * (g + 1))
                wait(pe, p_ok, g + 2 if not isinstance(g, int) else min(g + 2, NG))
                for b in range(GB):
                    last = product(ps_prob[:, b * NE:(b + 1) * NE],
                                   [(x2T[:, a, c, b * P:(b + 1) * P], G[w][:, c]) for c in range(DC) for a, w in PASSES])
                last.then_inc(gate_done, 1)

            def turn_x(g, par):
                pe.wait_ge(xn_ok, g + 1)
                for c in range(DC):
                    wait(pe, x2T_ok, 2 * (g - 3) + c + 1)
                    wait(pe, x_lo, DC * (g - 1) + c + 1)
                    for b in range(GB):
                        last = pe.transpose(ps_turn[c][:, b * P:(b + 1) * P], xn[:, b, c * P:(c + 1) * P], ident[:, :])
                    last.then_inc(x_turned, 1)

            def project_k(g, par):
                for f in range(DC):
                    pe.wait_ge(c_lo, DC * (g + 1))
                    wait(pe, q_ok, DC * (g - 1) + f + 1)
                    product(ps_proj[f][:, :], [(W[w][:, 1, c, f * P:(f + 1) * P], cT[:, a, c])
                                               for c in range(DC) for a, w in PASSES]).then_inc(k_done, 1)

            def project_v(g, par):
                for h in range(2):
                    pe.wait_ge(k_ok, DC * g + h + 1)
                    for b in (2 * h, 2 * h + 1):
                        last = product(ps_proj[h][:, (b % 2) * D:(b % 2 + 1) * D],
                                       [(cT[:, a, c, b * P:(b + 1) * P], W[w][:, 2, c]) for c in range(DC) for a, w in PASSES])
                    last.then_inc(v_done, 1)

            def project_q(g, par):
                pe.wait_ge(x_lo, DC * (g + 1))
                for f in range(DC):
                    pe.wait_ge(v_ok, 2 * g + f + 1)
                    product(ps_proj[f][:, :], [(W[w][:, 0, c, f * P:(f + 1) * P], xT[:, a, c])
                                               for c in range(DC) for a, w in PASSES]).then_inc(q_done, 1)

            def ranks(g, par):
                pe.wait_ge(route, ROUTE_OPS * g + SEL_AT)
                wait(pe, prob_ok, GB * (g + 3) if not isinstance(g, int) else GB * min(g + 3, NG))
                pe.matmul(ps_rank, before[:, :], sel[:, :, 0:NE], start=True, stop=False, skip_group_check=True)
                for b in range(GB - 1):
                    pe.matmul(ps_rank[:, (b + 1) * NE:], ones16[:, :], sel[:, b:b + 1, 0:NE].broadcast_to([P, GB - 1 - b, NE]),
                              start=False, stop=(b == GB - 2), skip_group_check=True)
                for b in range(GB):
                    last = pe.matmul(ps_total, ones16[:, :], sel[:, b, 0:NE], start=(b == 0), stop=(b == GB - 1), skip_group_check=True)
                last.then_inc(rank_done, 1)

            def step(at, t):
                at(1, scores)
                at(0, turn_x)
                at(0, project_k)
                at(1, turn_p)
                at(0, project_v)
                at(1, attend)
                at(3, ranks)
                at(0, project_q)
                at(2, turn_x2)
                at(2, gate)
            pipeline(pe, step)

            pe.wait_ge(table_ok, 1)

            def turn_tile(j, slot):
                par = slot % 2
                tile_arrived(pe, j, slot)
                wait(pe, xt_ok, j - 1)
                v = ps_xt[par][:, :].bitcast(F16).rearrange("p (h c t) -> p h c t", h=2, c=DC)
                for a in range(2):
                    for c in range(DC):
                        for b in range(TB):
                            last = pe.transpose(v[:, a, c, b * P:(b + 1) * P], tin[:, slot, b, a * D + c * P:a * D + (c + 1) * P], ident16[:, :])
                last.then_inc(t_turned, 1)

            def up(j, par, e):
                pe.wait_ge(xt_ok, j + 1)
                wait(pe, hid_ok, DC * (j - 1))
                for m, bank in enumerate((ps_h1[par], ps_h3[par])):
                    for i in range(DC):
                        at = m * D + i * P
                        last = product(bank[:, i * TR:(i + 1) * TR],
                                       [(wexp[:, bass.ds(e, 1), w, c * W13 + at:c * W13 + at + P].rearrange("p a f -> p (a f)"), xt[:, par, a, c])
                                        for c in range(DC) for a, w in PASSES])
                last.then_inc(h_done, 1)

            def down(j, par, e):
                pe.wait_ge(h_hi, j + 1)
                pe.wait_ge(h_lo, j + 1)
                wait(pe, ysum_ok, j - 1)
                for b in range(TB):
                    last = product(ps_y[par][:, b * D:(b + 1) * D],
                                   [(hT[:, par, a, c, b * P:(b + 1) * P],
                                     wexp[:, bass.ds(e, 1), w, DC * W13 + c * D:DC * W13 + (c + 1) * D].rearrange("p a f -> p (a f)"))
                                    for c in range(DC) for a, w in PASSES])
                last.then_inc(y_done, 1)

            def tile_step(j, slot, expert):
                if not isinstance(j, int) or j + 1 < NT:
                    turn_tile(j + 1, (slot + 1) % TS)
                up(j, slot % 2, expert(0))
                if not isinstance(j, int) or j:
                    down(j - 1, (slot + 1) % 2, expert(1))
            turn_tile(0, 0)
            tiles(pe, tile_step, last=True)
            down(NT - 1, 1, pe.value_load(tile_exp[0:1, NT - 1 + TS:NT + TS], min_val=0, max_val=NE - 1))


_OUTS = [((64, 128, 256), 'float32')]


def kernel(**inputs):
    import numpy as _np
    import concourse.bacc as _bacc
    from concourse import mybir as _mybir
    from concourse.bass_utils import run_bass_kernel_spmd as _run

    a = {k: _np.asarray(v) for k, v in inputs.items()}
    E, D = a['L0_ffn_Wg'].shape
    C = D // P

    def chunks(w):
        w = w.reshape(*w.shape[:-2], C, P, w.shape[-1])
        return _np.swapaxes(w, -3, -2).reshape(*w.shape[:-3], P, C * w.shape[-1])

    flip = lambda w: _np.swapaxes(w, -1, -2)
    up = _np.concatenate([flip(a['L0_ffn_W1']), flip(a['L0_ffn_W3'])], axis=-1)
    laid = {
        'x': a['x'],
        'ctxT': a['ctx_1024'].reshape(-1, GB * P, C, P).transpose(0, 3, 2, 1),
        'wqkv': _np.stack([chunks(a[f'L0_xattn_W{n}']).reshape(P, C, D) for n in 'qkv'], axis=1),
        'qk_bias': _np.stack([a['L0_xattn_bq'].reshape(C, P).T, a['L0_xattn_bk'].reshape(C, P).T], axis=1),
        'bv': a['L0_xattn_bv'],
        'wgT': chunks(a['L0_ffn_Wg'].T).reshape(P, C, E),
        'wexpT': _np.concatenate([chunks(up), chunks(flip(a['L0_ffn_W2']))], axis=-1),
        'b13': _np.stack([a[f'L0_ffn_b{n}'].reshape(E, C, P).transpose(2, 1, 0) for n in '13'], axis=1),
        'b2': a['L0_ffn_b2'],
    }
    nc = _bacc.Bacc("TRN2", target_bir_lowering=False, num_devices=1)
    arrays, args = {}, []
    for name, v in laid.items():
        v = _np.ascontiguousarray(v)
        arrays[f"in_{name}_dram"] = v
        args.append(nc.dram_tensor(f"in_{name}_dram", v.shape, _mybir.dt.from_np(v.dtype), kind="ExternalInput").ap())
    for i, (shape, dtype) in enumerate(_OUTS):
        dt = _mybir.dt.from_np(_np.dtype(dtype))
        args.append(nc.dram_tensor(f"out_{i}_dram", shape, dt, kind="ExternalOutput").ap())
    xattn_moe_kernel(nc, *args)
    r = _run(nc, [arrays], core_ids=[0])
    got = tuple(r.results[0][f"out_{i}_dram"] for i in range(len(_OUTS)))
    return got[0]
```

```python
from contextlib import ExitStack

import concourse.bass as bass
from concourse import mybir

F32 = mybir.dt.float32
F16 = mybir.dt.float16
I32 = mybir.dt.int32
ALU = mybir.AluOpType
ACT = mybir.ActivationFunctionType
AX_X = mybir.AxisListType.X

P = 128
GB = 4
TB = 2
TS = 4
WS = 32.0
EPS = 1e-5
TOPK, NGRP, TOPG, ROUTE_SCALE = 4, 4, 2, 2.5
SENTINEL = 9.0
STAGES = 4
REFINEMENTS = 3
PARTS = 2
SENT = 16


def xattn_moe_kernel(nc, x, ctxT, wqkv, qk_bias, bv, wgT, wexpT, b13, b2, out):
    B, S, D = x.shape
    NE = b2.shape[0]
    DC = D // P
    T = B * S
    NB = T // P
    NG = NB // GB
    GT = GB * P
    EG = NE // NGRP
    W13 = 2 * D
    WE = DC * W13 + DC * D
    TR = TB * P
    NT = T * TOPK // TR + NE
    REG = T + TR
    ROW = 2 * D + 4 * NE
    W_AT, TO_AT = D, D + NE
    SCORE_SCALE = 1.0 / (float(D) ** 0.5)
    assert S == P and DC == 2 and NG % 2 == 0 and NG >= 2 * STAGES and NE == NG and NT % TS == 0 and NE == 16

    x_rows = x.rearrange("(g b) s d -> g s b d", b=GB)
    rows_dram = nc.dram_tensor("expert_rows", [NE * REG + TR, ROW // 2], I32).ap()
    sums_dram = nc.dram_tensor("sums", [T + TR, D], F32).ap()
    x2_rows = sums_dram[0:T].rearrange("(g b s) d -> g s b d", b=GB, s=P)

    with ExitStack() as stack:
        def sb(name, shape, dt=F32):
            return stack.enter_context(nc.sbuf_tensor(name, shape, dt))

        def sem(name):
            return stack.enter_context(nc.semaphore(name))

        banks = [stack.enter_context(nc.psum_tensor(f"bank{i}", [P, 512], F32)) for i in range(8)]
        ps_turn = banks[0:2]
        ps_proj = banks[2:4]
        ps_score, ps_prob = banks[4], banks[5]
        ps_att = banks[6:8]
        ps_rank, ps_total = ps_score[:, 0:GB * NE], ps_score[:, GB * NE:(GB + 1) * NE]
        ps_xt = banks[0:2]
        ps_h1, ps_h3 = banks[2:4], banks[4:6]
        ps_y = banks[6:8]

        ident = sb("ident", [P, P])
        ident16 = sb("ident16", [P, P], F16)
        before = sb("before", [P, P], F16)
        ones16 = sb("ones16", [P, P], F16)
        carried_in = sb("carried_in", [P, 2])
        lower = sb("lower", [P, NGRP, NGRP])
        first_row = sb("first_row", [P, NE])
        token = sb("token", [P, NB])
        tile_no = sb("tile_no", [1, NT])
        pad_rows = sb("pad_rows", [P, TB, ROW], F16)

        whi = sb("whi", [P, 3, DC, D], F16)
        wlo = sb("wlo", [P, 3, DC, D], F16)
        qkb = sb("qkb", [P, 2, DC])
        bv_row = sb("bv_row", [1, 2, D], F16)
        wg_raw = sb("wg_raw", [P, DC, NE])
        wg_hi = sb("wg_hi", [P, DC, NE], F16)
        wg_lo = sb("wg_lo", [P, DC, NE], F16)
        stage = sb("stage", [P, 2, WE])
        wexp = sb("wexp", [P, NE, 2, WE], F16)
        b13s = sb("b13s", [P, 2, DC, NE])

        xin = sb("xin", [P, 2, GB, D])
        cin = sb("cin", [P, 2, DC, GT])
        xn = sb("xn", [P, GB, D])
        stat = sb("stat", [P, 2 * GB, 6])
        mean, dif, both, sq, shift = (sb(n, [P, 2 * GB]) for n in ("mean", "dif", "both", "sq", "shift"))
        veps = sb("veps", [P, 2 * GB])
        root = sb("root", [P, REFINEMENTS + 2, 2 * GB])
        square, slope = sb("square", [P, 2 * GB]), sb("slope", [P, 2 * GB])
        cT = sb("cT", [P, 2, DC, GT], F16)
        xT = sb("xT", [P, 2, DC, GT], F16)
        qT = sb("qT", [P, 2, DC, GT])
        kv = sb("kv", [P, 2, 2, DC * GT])
        kT = kv[:, 0].rearrange("p q (c t) -> p q c t", c=DC)
        vv = kv[:, 1].rearrange("p q (b d) -> p q b d", b=GB)
        wraw = kv[:, 0].rearrange("p q w -> p (q w)")[:, 0:3 * DC * D].rearrange("p (n c f) -> p n c f", n=3, c=DC)
        b2all = kv[:, :, :, :].rearrange("p a q w -> p (a q w)").rearrange("p (e d) -> p e d", e=NE)
        smax = sb("smax", [P, GB])
        nmax = sb("nmax", [P, GB])
        prob = sb("prob", [P, GB, P])
        bv_raw = prob[0:1].rearrange("p b k -> p (b k)")[:, 0:D]
        psums = sb("psums", [P, GB])
        rinv = sb("rinv", [P, GB])
        pT = sb("pT", [P, GB, P])
        x2 = sb("x2", [P, 2, GB, D])
        x2n = sb("x2n", [P, GB, D])
        rows = sb("rows", [P, 2, GB, ROW], F16)
        root_i, veps_i = root[:, :, :].bitcast(I32), veps[:, :].bitcast(I32)
        rows_f, rows_i = rows[:, :, :, :].bitcast(F32), rows[:, :, :, :].bitcast(I32)
        x2T = sb("x2T", [P, 2, DC, GT], F16)

        gexp = sb("gexp", [P, GB, NE])
        gden = sb("gden", [P, GB, NE])
        sig = sb("sig", [P, GB, NE])
        gmax = sb("gmax", [P, GB, NGRP])
        g_gt = sb("g_gt", [P, GB, NGRP, NGRP])
        g_eq = sb("g_eq", [P, GB, NGRP, NGRP])
        g_tie = sb("g_tie", [P, GB, NGRP, NGRP])
        g_beat = sb("g_beat", [P, GB, NGRP, NGRP])
        g_rank = sb("g_rank", [P, GB, NGRP])
        g_drop = sb("g_drop", [P, GB, NGRP])
        cand = sb("cand", [P, GB, NE + 4])
        top = sb("top", [P, GB, 8])
        want = sb("want", [P, GB, 8])
        left = sb("left", [P, GB, NE + 4])
        sel = sb("sel", [P, GB, NE], F16)
        share = sb("share", [P, GB, NE])
        wsum = sb("wsum", [P, GB])
        winv = sb("winv", [P, GB])
        rankb = sb("rankb", [P, GB, NE])
        key = sb("key", [P, GB, NE])
        top_key = sb("top_key", [P, GB, 8])
        row_at = sb("row_at", [P, 2, GB, TOPK], I32)
        next_row = sb("next_row", [P, NE])
        carrier = sb("carrier", [P, 1])
        pool_carrier = sb("pool_carrier", [P, 1])

        pad_to = sb("pad_to", [1, NE], I32)
        cnt = sb("cnt", [1, NE])
        cnt_i = sb("cnt_i", [1, NE], I32)
        tiles_i = sb("tiles_i", [1, NE], I32)
        tiles_f = sb("tiles_f", [1, NE])
        ends = sb("ends", [1, 5, 2 * NE])
        past = stage[:, :, :].rearrange("p q w -> p (q w)")[0:1, 0:NT * NE].rearrange("p (j e) -> p j e", j=NT)
        spare = x2T[:, :, :, :].rearrange("p h c t -> p (h c t)").bitcast(F32)[0:1, 0:4 * NT].rearrange("p (n j) -> p n j", n=4)
        tile_e, tile_b, tile_r, tile_s = (spare[:, k] for k in range(4))
        spare_i = xT[:, :, :, :].rearrange("p h c t -> p (h c t)").bitcast(I32)[0:1, 0:3 * (TS + NT)].rearrange("p (n j) -> p n j", n=3)
        tile_exp, tile_row, tile_first = (spare_i[:, k] for k in range(3))

        tin, tin_f, tin_i = (r[:, :, :, :].rearrange("p q (h b) w -> p (q h) b w", b=TB) for r in (rows, rows_f, rows_i))
        wt = sb("wt", [P, 2, TB, 2])
        y_to = sb("y_to", [P, 2, TB], I32)
        xt = cin[:, 1].rearrange("p c t -> p (c t)").bitcast(F16).rearrange("p (q h c t) -> p q h c t", q=2, h=2, c=DC)
        silu = xin[:, 0].rearrange("p b d -> p (b d)").rearrange("p (q c t) -> p q c t", q=2, c=DC)
        hid = xin[:, 1].rearrange("p b d -> p (b d)").rearrange("p (q c t) -> p q c t", q=2, c=DC)
        hT = cin[:, 0].rearrange("p c t -> p (c t)").bitcast(F16).rearrange("p (q h c t) -> p q h c t", q=2, h=2, c=DC)
        ysum = qT[:, 0].rearrange("p c t -> p (c t)").rearrange("p (q b d) -> p q b d", q=2, b=TB)
        yw = qT[:, 1].rearrange("p c t -> p (c t)").rearrange("p (q b d) -> p q b d", q=2, b=TB)

        small_in = sem("small_in")
        const_ok, setup_ok, w_ok = sem("const_ok"), sem("setup_ok"), sem("w_ok")
        b2_ok, b2_scaled = sem("b2_ok"), sem("b2_scaled")
        x_in, c_in, e_in = ([sem(f"{n}{k}") for k in range(2)] for n in ("x_in", "c_in", "e_in"))
        x_again, x2_out, rows_out = ([sem(f"{n}{k}") for k in range(2)] for n in ("x_again", "x2_out", "rows_out"))
        stat_ok, stat2_ok, root_ok = sem("stat_ok"), sem("stat2_ok"), sem("root_ok")
        xn_ok = sem("xn_ok")
        c_hi, c_lo, x_turned, x_hi, x_lo = sem("c_hi"), sem("c_lo"), sem("x_turned"), sem("x_hi"), sem("x_lo")
        k_done, k_ok, v_done, v_ok, q_done, q_ok = sem("k_done"), sem("k_ok"), sem("v_done"), sem("v_ok"), sem("q_done"), sem("q_ok")
        e_hi, e_lo = sem("e_hi"), sem("e_lo")
        score_done, smax_ok, nmax_ok, prob_ok = sem("score_done"), sem("smax_ok"), sem("nmax_ok"), sem("prob_ok")
        rinv_ok, p_turned, p_ok, att_done, x2_ok = sem("rinv_ok"), sem("p_turned"), sem("p_ok"), sem("att_done"), sem("x2_ok")
        x2n_ok, row_hi, row_lo = sem("x2n_ok"), sem("row_hi"), sem("row_lo")
        x2_turned, x2T_ok, gate_done, gexp_ok = sem("x2_turned"), sem("x2T_ok"), sem("gate_done"), sem("gexp_ok")
        route, rank_done, carried = sem("route"), sem("rank_done"), sem("carried")
        pad_in, spare_in, table, pad_ok, table_ok = sem("pad_in"), sem("spare_in"), sem("table"), sem("pad_ok"), sem("table_ok")
        t_in = [sem(f"t_in{k}") for k in range(TS)]
        wt_ok = sem("wt_ok")
        t_turned, xt_ok, h_done, silu_ok, hid_ok = sem("t_turned"), sem("xt_ok"), sem("h_done"), sem("silu_ok"), sem("hid_ok")
        h_hi, h_lo, y_done, ysum_ok, yw_ok, to_ok = sem("h_hi"), sem("h_lo"), sem("y_done"), sem("ysum_ok"), sem("yw_ok"), sem("to_ok")
        y_out = [sem("y_out0"), sem("y_out1")]
        copied = [sem("copied0"), sem("copied1")]

        SEL_AT, READ_AT, ROUTE_OPS = 18, 24, 27
        ROOT_OPS = 8 + 3 * REFINEMENTS

        def wait(eng, s, value):
            if isinstance(value, int) and value <= 0:
                return
            eng.wait_ge(s, value)

        def arrived(eng, sems, g, par, per=16):
            eng.wait_ge(sems[par], per * (g // 2 + 1) if isinstance(g, int) else (per // 2) * (g - par) + per)

        def settled(eng, sems, g, par, per=16):
            if isinstance(g, int):
                wait(eng, sems[par], per * (g // 2))
            else:
                eng.wait_ge(sems[par], (per // 2) * (g - par))

        def pipeline(eng, step):
            def run(t, odd):
                def at(s, f):
                    if not isinstance(t, int) or 0 <= t - s < NG:
                        f(t - s, (odd + s) % 2)
                step(at, t)
            for t in range(-1, STAGES + 2):
                run(t, t % 2)
            with eng.Fori(STAGES // 2 + 1, NG // 2 - 1) as i:
                run(2 * i, 0)
                run(2 * i + 1, 1)
            for t in range(NG - 2, NG + STAGES - 1):
                run(t, t % 2)

        def tiles(eng, body, first=True, last=False, with_experts=True):
            rounds = []

            def round_(j0):
                if with_experts:
                    regs = [eng.alloc_register(f"expert{n}_{len(rounds)}") for n in range(2 * TS)]
                    rounds.append(j0)
                    eng.load(regs, tile_exp[0:1, bass.ds(j0, 2 * TS)])
                    experts = [eng.snap(reg, donate=True, min_val=0, max_val=NE - 1) for reg in regs]
                for k in range(TS):
                    body(j0 + k, k, (lambda n, k=k: experts[TS + k - n]) if with_experts else None)
            if first:
                round_(0)
            with eng.Fori(int(first), NT // TS - int(last)) as i:
                round_(TS * i)
            if last:
                round_(NT - TS)

        def tile_arrived(eng, j, slot):
            eng.wait_ge(t_in[slot], 16 * (j // TS + 1) if isinstance(j, int) else (16 // TS) * (j - slot) + 16)

        def sent(eng, j, par):
            if isinstance(j, int):
                eng.wait_ge(y_out[par], SENT * TB * (j // 2) + SENT)
            else:
                eng.wait_ge(y_out[par], (SENT * TB // 2) * (j - par) + SENT)

        def copy_out(eng, part):
            for par in range(2):
                eng.wait_ge(y_out[par], SENT * TB * NT // 2 + SENT)
            for n in range(part * PARTS, (part + 1) * PARTS):
                rows_ = slice(n * T // (2 * PARTS), (n + 1) * T // (2 * PARTS))
                eng.dma_start(out.rearrange("b s d -> (b s) d")[rows_, :], sums_dram[rows_, :]).then_inc(copied[part], SENT)
            eng.wait_ge(copied[part], SENT * PARTS)

        block = stack.enter_context(nc.Block())

        @block.sync
        def _(sp):
            sp.dma_start(wraw, wqkv).then_inc(small_in, 16)
            sp.dma_start(qkb[:, :, :], qk_bias).then_inc(small_in, 16)
            sp.dma_start(wg_raw[:, :, :], wgT).then_inc(small_in, 16)
            sp.dma_start(b13s[:, :, :, :], b13).then_inc(small_in, 16)
            sp.dma_start(bv_raw, bv.rearrange("(a d) -> a d", a=1)).then_inc(small_in, 16)

            def load(g, par):
                wait(sp, c_lo, DC * (g - 1))
                sp.dma_start(cin[:, par], ctxT[g]).then_inc(c_in[par], 16)
                wait(sp, xn_ok, g - 1)
                sp.dma_start(xin[:, par], x_rows[g]).then_inc(x_in[par], 16)
                wait(sp, e_lo, g - 1)
                sp.dma_start(stage[:, par], wexpT[g]).then_inc(e_in[par], 16)
                if isinstance(g, int) and g == 1:
                    sp.wait_ge(setup_ok, 1)
                    sp.dma_start(rows_dram[NE * REG:NE * REG + TR, :].rearrange("(b p) w -> p b w", p=P),
                                 pad_rows[:, :, :].bitcast(I32)).then_inc(spare_in, 16)

            def load_again(g, par):
                settled(sp, x2_out, g, par)
                wait(sp, x2n_ok, GB * (g - 1))
                sp.dma_start(x2[:, par], x_rows[g]).then_inc(x_again[par], 16)

            def store(g, par):
                sp.wait_ge(x2_ok, GB * (g + 1))
                sp.dma_start(x2_rows[g], x2[:, par]).then_inc(x2_out[par], 16)

            def step(at, t):
                at(-1, load)
                at(0, load_again)
                at(1, store)
            pipeline(sp, step)
            sp.wait_ge(pad_ok, 1)
            for e in range(NE):
                row = sp.value_load(pad_to[0:1, e:e + 1], min_val=0, max_val=NE * REG)
                sp.dma_start(rows_dram[bass.ds(row, TR), :].rearrange("(b p) w -> p b w", p=P),
                             pad_rows[:, :, :].bitcast(I32)).then_inc(pad_in, 16)
            for par in range(2):
                sp.wait_ge(x2_out[par], 16 * NG // 2)

            sp.wait_ge(table_ok, 1)
            sp.wait_ge(spare_in, 16)
            sp.wait_ge(pad_in, 16 * NE)
            for par in range(2):
                sp.wait_ge(rows_out[par], 16 * GB * TOPK * NG // 2)

            def load_tile(j, slot, _):
                row = sp.value_load(tile_row[0:1, bass.ds(j + TS, 1)], min_val=0, max_val=NE * REG)
                wait(sp, t_turned, j - TS + 1)
                wait(sp, wt_ok, j - TS + 1)
                sp.dma_start(tin_i[:, slot], rows_dram[bass.ds(row, TR), :].rearrange("(b p) w -> p b w", p=P)).then_inc(t_in[slot], 16)
            tiles(sp, load_tile, with_experts=False)

            copy_out(sp, 0)

        @block.gpsimd
        def _(pool):
            n = [0]

            def const(ins):
                n[0] += 1
                ins.then_inc(const_ok, 1)
            pad_f = pad_rows[:, :, :].bitcast(F32)
            const(pool.memset(ident[:, :], 0.0))
            const(pool.memset(before[:, :], 1.0))
            const(pool.memset(lower[:, :, :], 1.0))
            const(pool.memset(ones16[:, :], 1.0))
            const(pool.memset(carried_in[:, :], 0.0))
            const(pool.memset(pad_f[:, :, 0:TO_AT], 0.0))
            const(pool.iota(pad_f[:, :, TO_AT:TO_AT + NE], [[P, TB], [0, NE]], base=T, channel_multiplier=1,
                            allow_small_or_imprecise_dtypes=True))
            const(pool.iota(first_row[:, :], [[1, NE]], base=0, channel_multiplier=0, allow_small_or_imprecise_dtypes=True))
            const(pool.iota(token[:, :], [[P, NB]], base=0, channel_multiplier=1, allow_small_or_imprecise_dtypes=True))
            const(pool.iota(tile_no[:, :], [[1, NT]], base=0, channel_multiplier=0, allow_small_or_imprecise_dtypes=True))
            pool.wait_ge(const_ok, n[0])
            const(pool.affine_select(out=ident[:, :], in_=ident[:, :], compare_op=ALU.not_equal, fill=1.0, base=0,
                                     pattern=[[-1, P]], channel_multiplier=1))
            const(pool.affine_select(out=before[:, :], in_=before[:, :], compare_op=ALU.is_gt, fill=0.0, base=0,
                                     pattern=[[1, P]], channel_multiplier=-1))
            const(pool.affine_select(out=lower[:, :, :], in_=lower[:, :, :], compare_op=ALU.is_gt, fill=0.0, base=0,
                                     pattern=[[1, NGRP], [-1, NGRP]], channel_multiplier=0))
            const(pool.tensor_scalar(first_row[:, :], first_row[:, :], float(REG), 1.0, ALU.mult, ALU.add))
            pool.wait_ge(const_ok, n[0])
            pool.tensor_copy(ident16[:, :], ident[:, :]).then_inc(setup_ok, 1)
            for b in range(TB):
                pool.dma_start(sums_dram[T + b * P:T + (b + 1) * P, :], pad_f[:, b, 0:D]).then_inc(y_out[b], SENT)

            def carry(k):
                wait(pool, carried, k)
                pool.tensor_tensor(pool_carrier[:, :], carried_in[:, 0:1], carried_in[:, 1:2], ALU.add).then_inc(carried, 1)

            def scatter(g, par):
                pool.wait_ge(route, ROUTE_OPS * (g + 1))
                pool.wait_ge(row_lo, g + 1)
                carry(g)
                for b in range(GB):
                    for k in range(TOPK):
                        pool.indirect_dma_start(rows_dram, bass.IndirectOffsetOnAxis(ap=row_at[:, par, b, k:k + 1], axis=0),
                                                rows_i[:, par, b], None).then_inc(rows_out[par], 16)

            def step(at, t):
                at(3, scatter)
            pipeline(pool, step)

            def send(j, slot, _):
                par = slot % 2
                first = pool.value_load(tile_first[0:1, bass.ds(j + TS, 1)], min_val=0, max_val=NT)
                pool.wait_ge(y_out[0], SENT * TB * ((first + 1) // 2) + SENT)
                pool.wait_ge(y_out[1], SENT * TB * (first // 2) + SENT)
                pool.wait_ge(to_ok, j + 1)
                pool.wait_ge(yw_ok, TB * (j + 1))
                carry(j + NG)
                for b in range(TB):
                    pool.indirect_dma_start(sums_dram, bass.IndirectOffsetOnAxis(ap=y_to[:, par, b:b + 1], axis=0),
                                            yw[:, par, b], None, compute_op=ALU.add).then_inc(y_out[par], SENT)
            pool.wait_ge(table_ok, 1)
            tiles(pool, send, first=False, with_experts=False)
            for par in range(2):
                pool.wait_ge(y_out[par], SENT * TB * NT // 2 + SENT)

        @block.scalar
        def _(act):
            act.wait_ge(small_in, 16 * 5)
            act.mul(whi[:, :, :, :], wraw, WS).then_inc(w_ok, 1)
            act.mul(wg_hi[:, :, :], wg_raw[:, :, :], WS).then_inc(w_ok, 1)
            act.mul(bv_row[:, 0], bv_raw, WS).then_inc(w_ok, 1)

            def norm(g, par):
                act.wait_ge(root_ok, ROOT_OPS * (g + 1))
                wait(act, x_turned, DC * g)
                for b in range(GB):
                    last = act.activation(xn[:, b], xin[:, par, b], ACT.Identity, bias=shift[:, b:b + 1],
                                          scale=root[:, REFINEMENTS, b:b + 1])
                last.then_inc(xn_ok, 1)

            def norm2(g, par):
                act.wait_ge(root_ok, ROOT_OPS * (g + 3))
                wait(act, row_lo, g)
                for b in range(GB):
                    act.activation(x2n[:, b], x2[:, par, b], ACT.Identity, bias=shift[:, GB + b:GB + b + 1],
                                   scale=root[:, REFINEMENTS, GB + b:GB + b + 1]).then_inc(x2n_ok, 1)

            def values(g, par):
                for c in range(2):
                    act.wait_ge(v_done, 2 * g + c + 1)
                    wait(act, att_done, 2 * (g - 1))
                    act.mul(vv[:, par, 2 * c:2 * c + 2], ps_proj[c][:, :].rearrange("p (b f) -> p b f", b=2), 1.0 / WS).then_inc(v_ok, 1)

            def split_c(g, par):
                arrived(act, c_in, g, par)
                for c in range(DC):
                    wait(act, v_done, 2 * g)
                    act.copy(cT[:, 0, c], cin[:, par, c]).then_inc(c_hi, 1)

            def split_e(g, par):
                arrived(act, e_in, g, par)
                act.mul(wexp[:, bass.ds(g, 1), 0, :].rearrange("p a w -> p (a w)"), stage[:, par], WS).then_inc(e_hi, 1)

            def split_x(g, par):
                for c in range(DC):
                    act.wait_ge(x_turned, DC * g + c + 1)
                    wait(act, q_done, DC * g)
                    act.copy(xT[:, 0, c], ps_turn[c][:, :]).then_inc(x_hi, 1)

            def keys(g, par):
                for c in range(DC):
                    act.wait_ge(k_done, DC * g + c + 1)
                    wait(act, score_done, g - 1)
                    act.activation(kT[:, par, c], ps_proj[c][:, :], ACT.Identity, bias=qkb[:, 1, c:c + 1], scale=1.0 / WS).then_inc(k_ok, 1)

            def queries(g, par):
                for c in range(DC):
                    act.wait_ge(q_done, DC * g + c + 1)
                    act.activation(qT[:, par, c], ps_proj[c][:, :], ACT.Identity, bias=qkb[:, 0, c:c + 1], scale=1.0 / WS).then_inc(q_ok, 1)

            def exponentials(g, par):
                act.wait_ge(nmax_ok, g + 1)
                wait(act, p_turned, g)
                wait(act, rinv_ok, g)
                for b in range(GB):
                    act.activation(prob[:, b], ps_score[:, b * P:(b + 1) * P], ACT.Exp, bias=nmax[:, b:b + 1],
                                   scale=SCORE_SCALE, accum_out=psums[:, b:b + 1]).then_inc(prob_ok, 1)

            def copy_p(g, par):
                act.wait_ge(p_turned, g + 1)
                wait(act, att_done, 2 * g)
                act.copy(pT[:, :, :], ps_prob[:, :].rearrange("p (b q) -> p b q", b=GB)).then_inc(p_ok, 1)

            def row_halves(g, par):
                act.wait_ge(x2n_ok, GB * (g + 1))
                settled(act, rows_out, g, par, 16 * GB * TOPK)
                act.copy(rows[:, par, :, 0:D], x2n[:, :, :]).then_inc(row_hi, 1)

            def copy_x2T(g, par):
                for h in range(2):
                    act.wait_ge(x2_turned, 2 * g + h + 1)
                    wait(act, gate_done, g)
                    act.copy(x2T[:, :, :, h * 2 * P:(h + 1) * 2 * P],
                             ps_turn[h][:, :].bitcast(F16).rearrange("p (h c t) -> p h c t", h=2, c=DC)).then_inc(x2T_ok, 1)

            def gate(g, par):
                act.wait_ge(gate_done, g + 1)
                wait(act, route, ROUTE_OPS * (g - 1) + SEL_AT)
                act.activation(gexp[:, :, :], ps_prob[:, 0:GB * NE].rearrange("p (b e) -> p b e", b=GB), ACT.Exp,
                               scale=-1.0 / WS).then_inc(gexp_ok, 1)

            def step(at, t):
                at(1, exponentials)
                at(0, keys)
                at(1, copy_p)
                at(0, norm)
                at(2, norm2)
                at(0, split_x)
                at(2, row_halves)
                at(0, values)
                at(-1, split_c)
                at(0, queries)
                at(2, copy_x2T)
                at(2, gate)
                at(-1, split_e)
            pipeline(act, step)

            act.wait_ge(score_done, NG)
            act.wait_ge(att_done, 2 * NG)
            act.dma_start(b2all.rearrange("p e d -> p (e d)"),
                          b2.rearrange("(a e) d -> a (e d)", a=1).broadcast_to([P, NE * D])).then_inc(b2_ok, 16)
            act.wait_ge(b2_ok, 16)
            act.mul(b2all, b2all, WS * WS).then_inc(b2_scaled, 1)
            act.wait_ge(table_ok, 1)

            def hidden(j, slot, e):
                par = slot % 2
                act.wait_ge(h_done, j + 1)
                wait(act, hid_ok, DC * (j - 1))
                for c in range(DC):
                    act.activation(silu[:, par, c], ps_h1[par][:, c * TR:(c + 1) * TR], ACT.Silu,
                                   bias=b13s[:, 0, c, bass.ds(e, 1)], scale=1.0 / WS).then_inc(silu_ok, 1)

            def copy_wt(j, slot, e):
                tile_arrived(act, j, slot)
                wait(act, yw_ok, TB * (j - 1))
                wait(act, to_ok, j - 1)
                act.copy(wt[:, slot % 2], tin_f[:, slot, :, W_AT:W_AT + 2 * NE].rearrange("p b (s e) -> p b s e", e=NE)
                         [:, :, :, bass.ds(e, 1)].rearrange("p b s a -> p b (s a)")).then_inc(wt_ok, 1)

            def high(j, slot):
                act.wait_ge(hid_ok, DC * (j + 1))
                wait(act, y_done, j - 1)
                act.copy(hT[:, slot % 2, 0], hid[:, slot % 2]).then_inc(h_hi, 1)

            def weigh(j, par):
                act.wait_ge(wt_ok, j + 1)
                act.wait_ge(ysum_ok, j + 1)
                sent(act, j, par)
                for b in range(TB):
                    act.mul(yw[:, par, b], ysum[:, par, b], wt[:, par, b, 0:1]).then_inc(yw_ok, 1)

            def tile_step(j, slot, expert):
                hidden(j, slot, expert(0))
                if not isinstance(j, int) or j >= 2:
                    weigh(j - 2, slot % 2)
                copy_wt(j, slot, expert(0))
                high(j, slot)
            tiles(act, tile_step)
            weigh(NT - 2, 0)
            weigh(NT - 1, 1)

            copy_out(act, 1)

        @block.vector
        def _(dve):
            dve.memset(cand[:, :, NE:NE + 4], SENTINEL)
            dve.memset(want[:, :, 4:8], SENTINEL)
            dve.memset(stat[:, :, :], 0.0)
            dve.memset(ends[:, :, :], 0.0).then_inc(w_ok, 1)
            dve.wait_ge(small_in, 16 * 5)
            dve.wait_ge(w_ok, 4)
            dve.tensor_scalar(b13s[:, 1], b13s[:, 1], WS, None, ALU.mult).then_inc(w_ok, 1)
            for lo, raw, hi in ((wlo[:, :, :, :].rearrange("p n c f -> p (n c f)"), wraw.rearrange("p n c f -> p (n c f)"),
                                 whi[:, :, :, :].rearrange("p n c f -> p (n c f)")),
                                (wg_lo[:, :, :].rearrange("p c e -> p (c e)"), wg_raw[:, :, :].rearrange("p c e -> p (c e)"),
                                 wg_hi[:, :, :].rearrange("p c e -> p (c e)")),
                                (bv_row[:, 1], bv_raw, bv_row[:, 0])):
                dve.scalar_tensor_tensor(out=lo, in0=raw, scalar=WS, in1=hi, op0=ALU.mult, op1=ALU.subtract).then_inc(w_ok, 1)
            dve.wait_ge(setup_ok, 1)
            dve.tensor_copy(next_row[:, :], first_row[:, :]).then_inc(w_ok, 1)

            def stats(g, par):
                arrived(dve, x_in, g, par)
                for b in range(GB):
                    dve.bn_stats(stat[:, b], xin[:, par, b]).then_inc(stat_ok, 1)

            def stats2(g, par):
                dve.wait_ge(x2_ok, GB * (g + 1))
                for b in range(GB):
                    dve.bn_stats(stat[:, GB + b], x2[:, par, b]).then_inc(stat2_ok, 1)

            def inverse_deviations(t):
                ops = [0]

                def seq(ins):
                    ops[0] += 1
                    ins.then_inc(root_ok, 1)

                def settle():
                    dve.wait_ge(root_ok, ROOT_OPS * (t + 1) + ops[0])
                if not isinstance(t, int) or t + 1 < NG:
                    dve.wait_ge(stat_ok, GB * (t + 2))
                if not isinstance(t, int) or t >= 1:
                    dve.wait_ge(stat2_ok, GB * t)
                wait(dve, xn_ok, t + 1 if not isinstance(t, int) else min(t + 1, NG))
                wait(dve, x2n_ok, GB * (t - 1))
                seq(dve.tensor_tensor(dif[:, :], stat[:, :, 1], stat[:, :, 4], ALU.subtract))
                seq(dve.scalar_tensor_tensor(out=both[:, :], in0=stat[:, :, 2], scalar=EPS * D, in1=stat[:, :, 5],
                                             op0=ALU.add, op1=ALU.add))
                yield
                settle()
                seq(dve.scalar_tensor_tensor(out=mean[:, :], in0=dif[:, :], scalar=0.5, in1=stat[:, :, 4], op0=ALU.mult, op1=ALU.add))
                seq(dve.scalar_tensor_tensor(out=sq[:, :], in0=dif[:, :], scalar=0.25, in1=dif[:, :], op0=ALU.mult, op1=ALU.mult))
                yield
                settle()
                seq(dve.scalar_tensor_tensor(out=veps[:, :], in0=both[:, :], scalar=1.0 / D, in1=sq[:, :], op0=ALU.mult, op1=ALU.add))
                yield
                settle()
                seq(dve.tensor_scalar(root_i[:, REFINEMENTS + 1], veps_i, 1, None, ALU.arith_shift_right))
                yield
                settle()
                seq(dve.tensor_scalar(root_i[:, 0], root_i[:, REFINEMENTS + 1], -1.0, float(0x5F3759DF), ALU.mult, ALU.add))
                for k in range(REFINEMENTS):
                    yield
                    settle()
                    seq(dve.scalar_tensor_tensor(out=square[:, :], in0=root[:, k], scalar=-0.5, in1=root[:, k], op0=ALU.mult, op1=ALU.mult))
                    yield
                    settle()
                    seq(dve.tensor_tensor(slope[:, :], square[:, :], veps[:, :], ALU.mult))
                    yield
                    settle()
                    seq(dve.scalar_tensor_tensor(out=root[:, k + 1], in0=slope[:, :], scalar=1.5, in1=root[:, k], op0=ALU.add, op1=ALU.mult))
                yield
                settle()
                seq(dve.scalar_tensor_tensor(out=shift[:, :], in0=mean[:, :], scalar=-1.0, in1=root[:, REFINEMENTS], op0=ALU.mult, op1=ALU.mult))
                assert ops[0] == ROOT_OPS, ops[0]

            def split_c(g, par):
                for c in range(DC):
                    dve.wait_ge(c_hi, DC * g + c + 1)
                    dve.tensor_tensor(cT[:, 1, c], cin[:, par, c], cT[:, 0, c], ALU.subtract).then_inc(c_lo, 1)

            def split_x(g, par):
                for c in range(DC):
                    dve.wait_ge(x_hi, DC * g + c + 1)
                    dve.tensor_tensor(xT[:, 1, c], ps_turn[c][:, :], xT[:, 0, c], ALU.subtract).then_inc(x_lo, 1)

            def split_e(g, par):
                dve.wait_ge(e_hi, g + 1)
                dve.scalar_tensor_tensor(out=wexp[:, bass.ds(g, 1), 1, :].rearrange("p a w -> p (a w)"), in0=stage[:, par], scalar=WS,
                                         in1=wexp[:, bass.ds(g, 1), 0, :].rearrange("p a w -> p (a w)"),
                                         op0=ALU.mult, op1=ALU.subtract).then_inc(e_lo, 1)

            def maxima(g, par):
                dve.wait_ge(score_done, g + 1)
                dve.tensor_reduce(smax[:, :], ps_score[:, :].rearrange("p (b k) -> p b k", b=GB), AX_X, ALU.max).then_inc(smax_ok, 1)
                dve.wait_ge(smax_ok, g + 1)
                wait(dve, prob_ok, GB * g)
                dve.tensor_scalar(nmax[:, :], smax[:, :], -SCORE_SCALE, None, ALU.mult).then_inc(nmax_ok, 1)

            def residual(g, par):
                dve.wait_ge(prob_ok, GB * (g + 1))
                dve.reciprocal(rinv[:, :], psums[:, :]).then_inc(rinv_ok, 1)
                dve.wait_ge(rinv_ok, g + 1)
                arrived(dve, x_again, g, par)
                for b in range(GB):
                    dve.wait_ge(att_done, 2 * g + b // 2 + 1)
                    dve.scalar_tensor_tensor(out=x2[:, par, b], in0=ps_att[b // 2][:, (b % 2) * D:(b % 2 + 1) * D],
                                             scalar=rinv[:, b:b + 1], in1=x2[:, par, b],
                                             op0=ALU.mult, op1=ALU.add).then_inc(x2_ok, 1)

            def row_halves(g, par):
                dve.wait_ge(row_hi, g + 1)
                dve.tensor_tensor(rows[:, par, :, D:2 * D], x2n[:, :, :], rows[:, par, :, 0:D], ALU.subtract).then_inc(row_lo, 1)

            n = [0]

            def seq(ins):
                n[0] += 1
                return ins.then_inc(route, 1)

            def settle(g):
                dve.wait_ge(route, ROUTE_OPS * g + n[0])

            def choose(g, par):
                n[0] = 0
                dve.wait_ge(gexp_ok, g + 1)
                seq(dve.tensor_scalar(gden[:, :, :], gexp[:, :, :], 1.0, None, ALU.add))
                yield
                settle(g)
                seq(dve.reciprocal(sig[:, :, :], gden[:, :, :]))
                yield
                settle(g)
                seq(dve.tensor_reduce(gmax[:, :, :], sig[:, :, :].rearrange("p b (g e) -> p b g e", g=NGRP), AX_X, ALU.max))
                yield
                settle(g)
                mine = gmax[:, :, :].rearrange("p b (g a) -> p b g a", a=1).broadcast_to([P, GB, NGRP, NGRP])
                other = gmax[:, :, :].rearrange("p b (a h) -> p b a h", a=1).broadcast_to([P, GB, NGRP, NGRP])
                seq(dve.tensor_tensor(g_gt[:, :, :, :], other, mine, ALU.is_gt))
                seq(dve.tensor_tensor(g_eq[:, :, :, :], other, mine, ALU.is_equal))
                yield
                settle(g)
                low = lower[:, :, :].rearrange("p g (a h) -> p a g h", a=1).broadcast_to([P, GB, NGRP, NGRP])
                seq(dve.tensor_tensor(g_tie[:, :, :, :], g_eq[:, :, :, :], low, ALU.mult))
                yield
                settle(g)
                seq(dve.tensor_tensor(g_beat[:, :, :, :], g_tie[:, :, :, :], g_gt[:, :, :, :], ALU.add))
                yield
                settle(g)
                seq(dve.tensor_reduce(g_rank[:, :, :], g_beat[:, :, :, :], AX_X, ALU.add))
                yield
                settle(g)
                seq(dve.tensor_scalar(g_drop[:, :, :], g_rank[:, :, :], float(TOPG), -2.0, ALU.is_ge, ALU.mult))
                yield
                settle(g)
                seq(dve.tensor_tensor(cand[:, :, 0:NE].rearrange("p b (g e) -> p b g e", g=NGRP),
                                      sig[:, :, :].rearrange("p b (g e) -> p b g e", g=NGRP),
                                      g_drop[:, :, :].rearrange("p b (g a) -> p b g a", a=1).broadcast_to([P, GB, NGRP, EG]), ALU.add))
                yield
                settle(g)
                seq(dve.memset(carrier[:, :], 0.0))
                for b in range(GB):
                    last = dve.max(top[:, b], cand[:, b, 0:NE])
                seq(last)
                yield
                settle(g)
                seq(dve.tensor_copy(want[:, :, 0:TOPK], top[:, :, 0:TOPK]))
                seq(dve.tensor_reduce(wsum[:, :], top[:, :, 0:TOPK], AX_X, ALU.add))
                yield
                settle(g)
                seq(dve.memset(carrier[:, :], 0.0))
                for b in range(GB):
                    last = dve.match_replace(left[:, b], want[:, b], cand[:, b], -2.0 * SENTINEL)
                seq(last)
                seq(dve.reciprocal(winv[:, :], wsum[:, :]))
                yield
                settle(g)
                seq(dve.tensor_scalar(sel[:, :, :], left[:, :, 0:NE], -SENTINEL, None, ALU.is_lt))
                assert n[0] == SEL_AT, n[0]
                seq(dve.scalar_tensor_tensor(out=share[:, :, :], in0=sig[:, :, :], scalar=ROUTE_SCALE / (WS * WS),
                                             in1=winv[:, :].rearrange("p (b a) -> p b a", a=1).broadcast_to([P, GB, NE]),
                                             op0=ALU.mult, op1=ALU.mult))
                yield
                settle(g)
                seq(dve.tensor_tensor(rows_f[:, par, :, W_AT:W_AT + NE], share[:, :, :], sel[:, :, :], ALU.mult))
                seq(dve.tensor_copy(rows_f[:, par, :, TO_AT:TO_AT + NE],
                                    token[:, bass.ds(g * GB, GB)].rearrange("p (b a) -> p b a", a=1).broadcast_to([P, GB, NE])))

            def place(g, par):
                dve.wait_ge(rank_done, g + 1)
                seq(dve.tensor_tensor(rankb[:, :, :], ps_rank.rearrange("p (b e) -> p b e", b=GB),
                                      next_row[:, :].rearrange("p (a e) -> p a e", a=1).broadcast_to([P, GB, NE]), ALU.add))
                settle(g)
                seq(dve.tensor_tensor(key[:, :, :], rankb[:, :, :], sel[:, :, :], ALU.mult))
                seq(dve.tensor_tensor(next_row[:, :], next_row[:, :], ps_total, ALU.add))
                assert n[0] == READ_AT, n[0]
                settle(g)
                seq(dve.memset(carrier[:, :], 0.0))
                for b in range(GB):
                    last = dve.max(top_key[:, b], key[:, b])
                seq(last)
                settle(g)
                settled(dve, rows_out, g, par, 16 * GB * TOPK)
                seq(dve.tensor_scalar(row_at[:, par], top_key[:, :, 0:TOPK], -1.0, None, ALU.add))
                assert n[0] == ROUTE_OPS, n[0]

            def alternate(*chains):
                chains = list(chains)
                while chains:
                    chains = [chain for chain in chains if next(chain, chain) is not chain]

            def step(at, t):
                at(0, split_e)
                at(3, place)
                at(-1, stats)
                at(0, split_x)
                at(2, row_halves)
                at(1, residual)
                at(1, stats2)
                at(-1, split_c)
                at(0, maxima)
                chains = []
                if not isinstance(t, int) or t <= NG:
                    chains.append(inverse_deviations(t))
                at(2, lambda g, par: chains.append(choose(g, par)))
                alternate(*chains)
            pipeline(dve, step)

            n[0] = 0

            def tab(ins):
                n[0] += 1
                ins.then_inc(table, 1)
                dve.wait_ge(table, n[0])
            dve.wait_ge(route, ROUTE_OPS * NG)
            dve.tensor_scalar(pad_to[:, :], next_row[0:1, :], -1.0, None, ALU.add).then_inc(pad_ok, 1)
            tab(dve.tensor_tensor(cnt[:, :], next_row[0:1, :], first_row[0:1, :], ALU.subtract))
            tab(dve.tensor_scalar(cnt_i[:, :], cnt[:, :], float(TR - 1), None, ALU.add))
            tab(dve.tensor_scalar(tiles_i[:, :], cnt_i[:, :], TR.bit_length() - 1, None, ALU.arith_shift_right))
            tab(dve.tensor_copy(tiles_f[:, :], tiles_i[:, :]))
            tab(dve.tensor_copy(ends[:, 0, NE:2 * NE], tiles_f[:, :]))
            for k in range(4):
                tab(dve.tensor_tensor(ends[:, k + 1, NE:2 * NE], ends[:, k, NE:2 * NE],
                                      ends[:, k, NE - 2 ** k:2 * NE - 2 ** k], ALU.add))
            tab(dve.tensor_tensor(past[:, :, :], tile_no[:, :].rearrange("p (j a) -> p j a", a=1).broadcast_to([1, NT, NE]),
                                  ends[:, 4, NE:2 * NE].rearrange("p (a e) -> p a e", a=1).broadcast_to([1, NT, NE]), ALU.is_ge))
            tab(dve.tensor_reduce(tile_e, past[:, :, :], AX_X, ALU.add))
            tab(dve.tensor_tensor(past[:, :, :], past[:, :, :],
                                  tiles_f[:, :].rearrange("p (a e) -> p a e", a=1).broadcast_to([1, NT, NE]), ALU.mult))
            tab(dve.tensor_reduce(tile_b, past[:, :, :], AX_X, ALU.add))
            tab(dve.tensor_tensor(tile_r, tile_no[:, :], tile_b, ALU.subtract))
            tab(dve.scalar_tensor_tensor(out=tile_s, in0=tile_e, scalar=float(NE), in1=tile_r, op0=ALU.is_ge, op1=ALU.mult))
            tab(dve.tensor_tensor(tile_first[:, TS:TS + NT], tile_b, tile_s, ALU.add))
            tab(dve.tensor_scalar(tile_s, tile_e, float(REG), None, ALU.mult))
            tab(dve.scalar_tensor_tensor(out=tile_b, in0=tile_r, scalar=float(TR), in1=tile_s, op0=ALU.mult, op1=ALU.add))
            tab(dve.tensor_scalar(tile_row[:, TS:TS + NT], tile_b, float(NE * REG), None, ALU.min))
            tab(dve.memset(tile_exp[:, 0:TS], 0))
            dve.tensor_scalar(tile_exp[:, TS:TS + NT], tile_e, float(NE - 1), None, ALU.min).then_inc(table_ok, 1)
            dve.wait_ge(table_ok, 1)
            dve.wait_ge(b2_scaled, 1)

            def copy_xt(j, par):
                dve.wait_ge(t_turned, j + 1)
                wait(dve, h_done, j - 1)
                dve.tensor_copy(xt[:, par], ps_xt[par][:, :].bitcast(F16).rearrange("p (h c t) -> p h c t", h=2, c=DC)).then_inc(xt_ok, 1)

            def hidden(j, par, e):
                for c in range(DC):
                    dve.wait_ge(silu_ok, DC * j + c + 1)
                    if c == 0:
                        wait(dve, h_hi, j - 1)
                    dve.scalar_tensor_tensor(out=hid[:, par, c], in0=ps_h3[par][:, c * TR:(c + 1) * TR],
                                             scalar=b13s[:, 1, c, bass.ds(e, 1)], in1=silu[:, par, c],
                                             op0=ALU.add, op1=ALU.mult).then_inc(hid_ok, 1)

            def low_half(j, par):
                dve.wait_ge(h_hi, j + 1)
                dve.tensor_tensor(hT[:, par, 1], hid[:, par], hT[:, par, 0], ALU.subtract).then_inc(h_lo, 1)

            def results(j, par, e):
                dve.wait_ge(y_done, j + 1)
                wait(dve, yw_ok, TB * (j - 1))
                dve.tensor_tensor(ysum[:, par], ps_y[par][:, :].rearrange("p (b d) -> p b d", b=TB),
                                  b2all[:, bass.ds(e, 1), :].broadcast_to([P, TB, D]), ALU.add).then_inc(ysum_ok, 1)
                dve.wait_ge(wt_ok, j + 1)
                sent(dve, j, par)
                dve.tensor_copy(y_to[:, par], wt[:, par, :, 1]).then_inc(to_ok, 1)

            def tile_step(j, slot, expert):
                par = slot % 2
                done = not isinstance(j, int) or j >= 2
                if not isinstance(j, int) or j >= 1:
                    low_half(j - 1, 1 - par)
                if not isinstance(j, int) or j + 1 < NT:
                    copy_xt(j + 1, 1 - par)
                if done:
                    results(j - 2, par, expert(2))
                hidden(j, par, expert(0))
            copy_xt(0, 0)
            tiles(dve, tile_step, last=True)
            low_half(NT - 1, 1)
            for j in (NT - 2, NT - 1):
                results(j, j % 2, dve.value_load(tile_exp[0:1, j + TS:j + TS + 1], min_val=0, max_val=NE - 1))

        @block.tensor
        def _(pe):
            pe.wait_ge(setup_ok, 1)
            pe.wait_ge(w_ok, 9)
            PASSES = ((0, 0), (0, 1), (1, 0))
            W = (whi, wlo)
            G = (wg_hi, wg_lo)

            def product(out_ap, pairs):
                for k, (lhs, rhs) in enumerate(pairs):
                    last = pe.matmul(out_ap, lhs, rhs, start=(k == 0), stop=(k == len(pairs) - 1))
                return last

            def scores(g, par):
                pe.wait_ge(q_ok, DC * (g + 1))
                pe.wait_ge(k_ok, DC * (g + 1))
                wait(pe, prob_ok, GB * g)
                wait(pe, route, ROUTE_OPS * (g - 3) + READ_AT)
                for b in range(GB):
                    t = slice(b * P, (b + 1) * P)
                    last = product(ps_score[:, t], [(qT[:, par, c, t], kT[:, par, c, t]) for c in range(DC)])
                last.then_inc(score_done, 1)

            def turn_p(g, par):
                pe.wait_ge(prob_ok, GB * (g + 1))
                wait(pe, p_ok, g)
                wait(pe, gexp_ok, g - 1)
                for b in range(GB):
                    last = pe.transpose(ps_prob[:, b * P:(b + 1) * P], prob[:, b], ident[:, :])
                last.then_inc(p_turned, 1)

            def attend(g, par):
                pe.wait_ge(p_ok, g + 1)
                pe.wait_ge(v_ok, 2 * (g + 1))
                wait(pe, x2_ok, GB * g)
                for b in range(GB):
                    last = product(ps_att[b // 2][:, (b % 2) * D:(b % 2 + 1) * D], [(pT[:, b], vv[:, par, b])])
                    if b % 2:
                        last.then_inc(att_done, 1)

            def turn_x2(g, par):
                pe.wait_ge(row_hi, g + 1)
                pe.wait_ge(row_lo, g + 1)
                for h in range(2):
                    wait(pe, x_lo, DC * (g + 2) + h + 1 if not isinstance(g, int) else min(DC * (g + 2) + h + 1, DC * NG))
                    v = ps_turn[h][:, :].bitcast(F16).rearrange("p (h c t) -> p h c t", h=2, c=DC)
                    for b in range(2):
                        for a in range(2):
                            for c in range(DC):
                                last = pe.transpose(v[:, a, c, b * P:(b + 1) * P],
                                                    rows[:, par, 2 * h + b, a * D + c * P:a * D + (c + 1) * P], ident16[:, :])
                    last.then_inc(x2_turned, 1)

            def gate(g, par):
                pe.wait_ge(x2T_ok, 2 * (g + 1))
                wait(pe, p_ok, g + 2 if not isinstance(g, int) else min(g + 2, NG))
                for b in range(GB):
                    last = product(ps_prob[:, b * NE:(b + 1) * NE],
                                   [(x2T[:, a, c, b * P:(b + 1) * P], G[w][:, c]) for c in range(DC) for a, w in PASSES])
                last.then_inc(gate_done, 1)

            def turn_x(g, par):
                pe.wait_ge(xn_ok, g + 1)
                for c in range(DC):
                    wait(pe, x2T_ok, 2 * (g - 3) + c + 1)
                    wait(pe, x_lo, DC * (g - 1) + c + 1)
                    for b in range(GB):
                        last = pe.transpose(ps_turn[c][:, b * P:(b + 1) * P], xn[:, b, c * P:(c + 1) * P], ident[:, :])
                    last.then_inc(x_turned, 1)

            def project_k(g, par):
                for f in range(DC):
                    pe.wait_ge(c_lo, DC * (g + 1))
                    wait(pe, q_ok, DC * (g - 1) + f + 1)
                    product(ps_proj[f][:, :], [(W[w][:, 1, c, f * P:(f + 1) * P], cT[:, a, c])
                                               for c in range(DC) for a, w in PASSES]).then_inc(k_done, 1)

            def project_v(g, par):
                for h in range(2):
                    pe.wait_ge(k_ok, DC * g + h + 1)
                    for b in (2 * h, 2 * h + 1):
                        last = product(ps_proj[h][:, (b % 2) * D:(b % 2 + 1) * D],
                                       [(cT[:, a, c, b * P:(b + 1) * P], W[w][:, 2, c]) for c in range(DC) for a, w in PASSES]
                                       + [(ones16[0:1, :], bv_row[:, w]) for w in range(2)])
                    last.then_inc(v_done, 1)

            def project_q(g, par):
                pe.wait_ge(x_lo, DC * (g + 1))
                for f in range(DC):
                    pe.wait_ge(v_ok, 2 * g + f + 1)
                    product(ps_proj[f][:, :], [(W[w][:, 0, c, f * P:(f + 1) * P], xT[:, a, c])
                                               for c in range(DC) for a, w in PASSES]).then_inc(q_done, 1)

            def ranks(g, par):
                pe.wait_ge(route, ROUTE_OPS * g + SEL_AT)
                wait(pe, prob_ok, GB * (g + 3) if not isinstance(g, int) else GB * min(g + 3, NG))
                pe.matmul(ps_rank, before[:, :], sel[:, :, :], start=True, stop=False, skip_group_check=True)
                for b in range(GB - 1):
                    pe.matmul(ps_rank[:, (b + 1) * NE:], ones16[:, :], sel[:, b:b + 1, :].broadcast_to([P, GB - 1 - b, NE]),
                              start=False, stop=(b == GB - 2), skip_group_check=True)
                for b in range(GB):
                    last = pe.matmul(ps_total, ones16[:, :], sel[:, b, :], start=(b == 0), stop=(b == GB - 1), skip_group_check=True)
                last.then_inc(rank_done, 1)

            def step(at, t):
                at(0, project_k)
                at(1, turn_p)
                at(0, project_v)
                at(3, ranks)
                at(0, turn_x)
                at(1, attend)
                at(0, project_q)
                at(2, turn_x2)
                at(0, scores)
                at(2, gate)
            pipeline(pe, step)

            pe.wait_ge(table_ok, 1)

            def turn_tile(j, slot):
                par = slot % 2
                tile_arrived(pe, j, slot)
                wait(pe, xt_ok, j - 1)
                v = ps_xt[par][:, :].bitcast(F16).rearrange("p (h c t) -> p h c t", h=2, c=DC)
                for a in range(2):
                    for c in range(DC):
                        for b in range(TB):
                            last = pe.transpose(v[:, a, c, b * P:(b + 1) * P], tin[:, slot, b, a * D + c * P:a * D + (c + 1) * P], ident16[:, :])
                last.then_inc(t_turned, 1)

            def up(j, par, e):
                pe.wait_ge(xt_ok, j + 1)
                wait(pe, hid_ok, DC * (j - 1))
                for m, bank in enumerate((ps_h1[par], ps_h3[par])):
                    for i in range(DC):
                        at = m * D + i * P
                        last = product(bank[:, i * TR:(i + 1) * TR],
                                       [(wexp[:, bass.ds(e, 1), w, c * W13 + at:c * W13 + at + P].rearrange("p a f -> p (a f)"), xt[:, par, a, c])
                                        for c in range(DC) for a, w in PASSES])
                last.then_inc(h_done, 1)

            def down(j, par, e):
                pe.wait_ge(h_hi, j + 1)
                pe.wait_ge(h_lo, j + 1)
                wait(pe, ysum_ok, j - 1)
                for b in range(TB):
                    last = product(ps_y[par][:, b * D:(b + 1) * D],
                                   [(hT[:, par, a, c, b * P:(b + 1) * P],
                                     wexp[:, bass.ds(e, 1), w, DC * W13 + c * D:DC * W13 + (c + 1) * D].rearrange("p a f -> p (a f)"))
                                    for c in range(DC) for a, w in PASSES])
                last.then_inc(y_done, 1)

            def tile_step(j, slot, expert):
                if not isinstance(j, int) or j + 1 < NT:
                    turn_tile(j + 1, (slot + 1) % TS)
                up(j, slot % 2, expert(0))
                if not isinstance(j, int) or j:
                    down(j - 1, (slot + 1) % 2, expert(1))
            turn_tile(0, 0)
            tiles(pe, tile_step, last=True)
            down(NT - 1, 1, pe.value_load(tile_exp[0:1, NT - 1 + TS:NT + TS], min_val=0, max_val=NE - 1))


_OUTS = [((64, 128, 256), 'float32')]


def kernel(**inputs):
    import numpy as _np
    import concourse.bacc as _bacc
    from concourse import mybir as _mybir
    from concourse.bass_utils import run_bass_kernel_spmd as _run

    a = {k: _np.asarray(v) for k, v in inputs.items()}
    E, D = a['L0_ffn_Wg'].shape
    C = D // P

    def chunks(w):
        w = w.reshape(*w.shape[:-2], C, P, w.shape[-1])
        return _np.swapaxes(w, -3, -2).reshape(*w.shape[:-3], P, C * w.shape[-1])

    flip = lambda w: _np.swapaxes(w, -1, -2)
    up = _np.concatenate([flip(a['L0_ffn_W1']), flip(a['L0_ffn_W3'])], axis=-1)
    laid = {
        'x': a['x'],
        'ctxT': a['ctx_1024'].reshape(-1, GB * P, C, P).transpose(0, 3, 2, 1),
        'wqkv': _np.stack([chunks(a[f'L0_xattn_W{n}']).reshape(P, C, D) for n in 'qkv'], axis=1),
        'qk_bias': _np.stack([a['L0_xattn_bq'].reshape(C, P).T, a['L0_xattn_bk'].reshape(C, P).T], axis=1),
        'bv': a['L0_xattn_bv'],
        'wgT': chunks(a['L0_ffn_Wg'].T).reshape(P, C, E),
        'wexpT': _np.concatenate([chunks(up), chunks(flip(a['L0_ffn_W2']))], axis=-1),
        'b13': _np.stack([a[f'L0_ffn_b{n}'].reshape(E, C, P).transpose(2, 1, 0) for n in '13'], axis=1),
        'b2': a['L0_ffn_b2'],
    }
    nc = _bacc.Bacc("TRN2", target_bir_lowering=False, num_devices=1)
    arrays, args = {}, []
    for name, v in laid.items():
        v = _np.ascontiguousarray(v)
        arrays[f"in_{name}_dram"] = v
        args.append(nc.dram_tensor(f"in_{name}_dram", v.shape, _mybir.dt.from_np(v.dtype), kind="ExternalInput").ap())
    for i, (shape, dtype) in enumerate(_OUTS):
        dt = _mybir.dt.from_np(_np.dtype(dtype))
        args.append(nc.dram_tensor(f"out_{i}_dram", shape, dt, kind="ExternalOutput").ap())
    xattn_moe_kernel(nc, *args)
    r = _run(nc, [arrays], core_ids=[0])
    got = tuple(r.results[0][f"out_{i}_dram"] for i in range(len(_OUTS)))
    return got[0]
```
